# Optimizing a Trainium2 kernel written in Bass

```python
import numpy as np
import jax
import jax.numpy as jnp

def _softmax(x, axis=-1):
    return jax.nn.softmax(x, axis=axis)

def _gelu(x):
    return jax.nn.gelu(x, approximate=True)

def _silu(x):
    return jax.nn.silu(x)

def _sigmoid(x):
    return jax.nn.sigmoid(x)

def _layernorm(x, axis=-1, eps=1e-05):
    m = jnp.mean(x, axis=axis, keepdims=True)
    v = jnp.var(x, axis=axis, keepdims=True)
    return (x - m) / jnp.sqrt(v + eps)

def _scatter_add(tgt, idx, src, axis=0):
    return tgt.at[idx].add(src)

def _segment_sum(src, seg, n):
    return jax.ops.segment_sum(src, seg, n)
kernel_name = 'mk_gnn_preln_d1_gnn_r8_ee48ca'

def setup_inputs(seed: int=0):
    np.random.seed(seed)
    _w = jnp.asarray

    def _rec_inputs():
        import jax
        import jax.numpy as jnp
        _gk = jax.random.key(seed)
        x = -0.0005121 + 1.001 * jax.random.normal(jax.random.fold_in(_gk, 1), (6250, 64), jnp.float32)
        _s = jax.random.randint(jax.random.fold_in(_gk, 2), (100000,), 0, 6250, jnp.int32)
        _d = jax.random.randint(jax.random.fold_in(_gk, 3), (100000,), 0, 6250, jnp.int32)
        _loop = jnp.arange(6250, dtype=jnp.int32)
        src = jnp.concatenate([_s, _d, _loop])
        dst = jnp.concatenate([_d, _s, _loop])
        _o = jnp.argsort(dst, stable=True)
        src = src[_o]
        dst = dst[_o]
        edge_attr_16 = 0.000254156 + 0.999948 * jax.random.normal(jax.random.fold_in(_gk, 11), (206250, 16), jnp.float32)
        return (x, src, dst, edge_attr_16)
    x, src, dst, edge_attr_16 = _rec_inputs()

    def _L0_gnn_setup():
        import jax, jax.numpy as jnp
        import numpy as np
        N, E, F, ED, L = (6250, 100000, 64, 16, 2)
        EPS_BN = 1e-05

        def _layer(x, src, dst, edge_attr, We, be, Wpre, bpre, Wpost, bpost, Wlin, blin, gamma, beta):
            e = edge_attr @ We + be
            h = jnp.concatenate([x[src], e], axis=-1) @ Wpre + bpre
            cnt = jax.ops.segment_sum(jnp.ones(h.shape[0], h.dtype), dst, num_segments=N)
            safe_cnt = jnp.maximum(cnt, 1.0)
            mean = jax.ops.segment_sum(h, dst, num_segments=N) / safe_cnt[:, None]
            empty = (cnt == 0)[:, None]
            mn = jnp.where(empty, 0.0, jax.ops.segment_min(h, dst, num_segments=N))
            mx = jnp.where(empty, 0.0, jax.ops.segment_max(h, dst, num_segments=N))
            agg = jnp.concatenate([mean, mn, mx], axis=-1)
            deg_i = cnt.astype(jnp.int32)
            bc = jnp.bincount(deg_i, length=N).astype(h.dtype)
            avg_log = jnp.mean(jnp.log(bc + 1.0))
            amp = (jnp.log(safe_cnt + 1.0) / avg_log)[:, None]
            out = jnp.concatenate([agg, agg * amp], axis=-1)
            out = jnp.concatenate([x, out], axis=-1) @ Wpost + bpost
            out = out @ Wlin + blin
            mu = out.mean(axis=0)
            var = jnp.mean((out - mu) ** 2, axis=0)
            out = gamma * (out - mu) / jnp.sqrt(var + EPS_BN) + beta
            return jax.nn.relu(out)
        key = jax.random.key(seed)
        ks = jax.random.split(key, 8)
        s = 0.05
        return {'x': jax.random.normal(ks[0], (N, F), jnp.float32), 'edge_index': jax.random.randint(ks[1], (2, E), 0, N), 'edge_attr': jax.random.normal(ks[2], (E, ED), jnp.float32), 'We': jax.random.normal(ks[3], (L, ED, F), jnp.float32) * s, 'be': jnp.zeros((L, F), jnp.float32), 'Wpre': jax.random.normal(ks[4], (L, 2 * F, F), jnp.float32) * s, 'bpre': jnp.zeros((L, F), jnp.float32), 'Wpost': jax.random.normal(ks[5], (L, 7 * F, F), jnp.float32) * s, 'bpost': jnp.zeros((L, F), jnp.float32), 'Wlin': jax.random.normal(ks[6], (L, F, F), jnp.float32) * s, 'blin': jnp.zeros((L, F), jnp.float32), 'gamma': jnp.ones((L, F), jnp.float32), 'beta': jnp.zeros((L, F), jnp.float32)}
    _L0_gnn_all = _L0_gnn_setup()
    _L0_gnn_in = {k: v for k, v in _L0_gnn_all.items() if k in ('We', 'be', 'Wpre', 'bpre', 'Wpost', 'bpost', 'Wlin', 'blin', 'gamma', 'beta')}
    del _L0_gnn_all
    return {'x': x, 'src': src, 'dst': dst, 'edge_attr_16': edge_attr_16, 'L0_gnn_We': _L0_gnn_in['We'], 'L0_gnn_be': _L0_gnn_in['be'], 'L0_gnn_Wpre': _L0_gnn_in['Wpre'], 'L0_gnn_bpre': _L0_gnn_in['bpre'], 'L0_gnn_Wpost': _L0_gnn_in['Wpost'], 'L0_gnn_bpost': _L0_gnn_in['bpost'], 'L0_gnn_Wlin': _L0_gnn_in['Wlin'], 'L0_gnn_blin': _L0_gnn_in['blin'], 'L0_gnn_gamma': _L0_gnn_in['gamma'], 'L0_gnn_beta': _L0_gnn_in['beta']}

def reference(x, src, dst, edge_attr_16, L0_gnn_We, L0_gnn_be, L0_gnn_Wpre, L0_gnn_bpre, L0_gnn_Wpost, L0_gnn_bpost, L0_gnn_Wlin, L0_gnn_blin, L0_gnn_gamma, L0_gnn_beta):
    import jax
    import jax.numpy as jnp

    def _L0_gnn_ref(x, edge_index, edge_attr, We, be, Wpre, bpre, Wpost, bpost, Wlin, blin, gamma, beta):
        import jax, jax.numpy as jnp
        import numpy as np
        N, E, F, ED, L = (6250, 100000, 64, 16, 2)
        EPS_BN = 1e-05

        def _layer(x, src, dst, edge_attr, We, be, Wpre, bpre, Wpost, bpost, Wlin, blin, gamma, beta):
            e = edge_attr @ We + be
            h = jnp.concatenate([x[src], e], axis=-1) @ Wpre + bpre
            cnt = jax.ops.segment_sum(jnp.ones(h.shape[0], h.dtype), dst, num_segments=N)
            safe_cnt = jnp.maximum(cnt, 1.0)
            mean = jax.ops.segment_sum(h, dst, num_segments=N) / safe_cnt[:, None]
            empty = (cnt == 0)[:, None]
            mn = jnp.where(empty, 0.0, jax.ops.segment_min(h, dst, num_segments=N))
            mx = jnp.where(empty, 0.0, jax.ops.segment_max(h, dst, num_segments=N))
            agg = jnp.concatenate([mean, mn, mx], axis=-1)
            deg_i = cnt.astype(jnp.int32)
            bc = jnp.bincount(deg_i, length=N).astype(h.dtype)
            avg_log = jnp.mean(jnp.log(bc + 1.0))
            amp = (jnp.log(safe_cnt + 1.0) / avg_log)[:, None]
            out = jnp.concatenate([agg, agg * amp], axis=-1)
            out = jnp.concatenate([x, out], axis=-1) @ Wpost + bpost
            out = out @ Wlin + blin
            mu = out.mean(axis=0)
            var = jnp.mean((out - mu) ** 2, axis=0)
            out = gamma * (out - mu) / jnp.sqrt(var + EPS_BN) + beta
            return jax.nn.relu(out)
        src, dst = (edge_index[0], edge_index[1])
        for l in range(L):
            x = _layer(x, src, dst, edge_attr, We[l], be[l], Wpre[l], bpre[l], Wpost[l], bpost[l], Wlin[l], blin[l], gamma[l], beta[l])
        return x
    edge_index = jnp.stack([src, dst])
    h = jnp.maximum(_layernorm(x, axis=-1), 0.0)
    x = x + _L0_gnn_ref(h, edge_index, edge_attr_16, L0_gnn_We, L0_gnn_be, L0_gnn_Wpre, L0_gnn_bpre, L0_gnn_Wpost, L0_gnn_bpost, L0_gnn_Wlin, L0_gnn_blin, L0_gnn_gamma, L0_gnn_beta)
    return x

_drawn_inputs = setup_inputs


def setup_inputs(seed=0):
    import zlib

    import numpy as np

    out = dict(_drawn_inputs(seed))
    spreads = {'L0_gnn_be': (0.0, 0.505),
     'L0_gnn_bpre': (0.0, 0.1),
     'L0_gnn_bpost': (0.0, 0.8),
     'L0_gnn_blin': (0.0, 0.8),
     'L0_gnn_gamma': (1.0, 0.2),
     'L0_gnn_beta': (0.0, 0.1)}
    factors = {}
    for name, (base, spread) in spreads.items():
        noise = np.random.default_rng([zlib.crc32(name.encode()), seed]).standard_normal(out[name].shape)
        drawn = base * np.exp(spread * noise) if base else spread * noise
        out[name] = jnp.asarray(drawn.astype(out[name].dtype))
    for name, factor in factors.items():
        out[name] = (out[name] * factor).astype(out[name].dtype)
    return out
```

```python
import concourse.bass as bass
from concourse import mybir
from contextlib import ExitStack

P = 128
N, F, ED, LAYERS = 6250, 64, 16, 2
E = 206250
GC = 8
COLS = -(-E // (P * GC)) * GC
NG = COLS // GC
LASTC = E - (P - 1) * COLS
SLOTS = 4
NT = -(-N // P)
NL = N - (NT - 1) * P
CHUNK = 625
NCH = E // CHUNK
ZROW = P * COLS
SW = 3 * F
NEG = GC * ED
CW = NEG + 2 * GC
BIG = 1.0e38
EPS = 1e-5


def gnn_program(nc, x, src, dst, ea, We, be, Wpre, bpre, Wpost, bpost, Wlin, blin, gamma, beta, out):
    f32, i32 = mybir.dt.float32, mybir.dt.int32
    ALU = mybir.AluOpType
    ACT = mybir.ActivationFunctionType
    AX = mybir.AxisListType

    y_dram = nc.dram_tensor("y_rows", (N, F), f32, kind="Internal").ap()
    st_dram = nc.dram_tensor("edge_states", (ZROW + 1, SW), f32, kind="Internal").ap()

    ctx = ExitStack()
    with ctx:
        def sb(name, shape, dt=f32):
            return ctx.enter_context(nc.sbuf_tensor(name, shape, dt))

        def sem(name):
            return ctx.enter_context(nc.semaphore(name))

        comb = sb("comb", [P, NG, NEG + GC])
        src_all = sb("src_all", [P, COLS], i32)
        x_all = sb("x_all", [P, NT, F])
        o_all = sb("o_all", [P, NT, F])
        states = sb("states", [P, SLOTS, GC, SW])
        rows = sb("rows", [P, SLOTS * CHUNK])
        stage = sb("stage", [P, SLOTS, CW])
        idx = sb("idx", [P, SLOTS, GC], i32)
        eaT = sb("eaT", [P, 2, P])
        tsb = sb("tsb", [P, 2, 2 * P])
        xp = sb("xp", [P, SLOTS, 2 * F])
        ident = sb("ident", [P, P])
        ones = sb("ones", [P, P])
        shiftm = sb("shiftm", [P, P])
        wrapm = sb("wrapm", [P, P])
        bdmask = sb("bdmask", [P, GC])
        bd = sb("bd", [P, LAYERS, GC * F])
        bd1 = sb("bd1", [P, LAYERS, 2 * F])
        rw = sb("rw", [P, LAYERS, 4, F])
        w64 = sb("w64", [F, LAYERS, 2, F])
        we = sb("we", [ED, LAYERS, F])
        weT = sb("weT", [F, GC, ED])
        bcol = sb("bcol", [F, LAYERS, 2])
        brow = sb("brow", [1, LAYERS, 4, F])
        crow = sb("crow", [1, LAYERS, 3, F])
        gb = sb("gb", [P, LAYERS, 2, F])
        nid = sb("nid", [P, NT])
        nidh = sb("nidh", [P, NT])
        nidi = sb("nidi", [P, NT], i32)
        le = sb("le", [P, NT])
        chrow = sb("chrow", [P, NT])
        chrow_i = sb("chrow_i", [P, NT], i32)
        sg = sb("sg", [P, NT])
        ends = sb("ends", [P, NT])
        deg = sb("deg", [P, NT])
        cnt = sb("cnt", [P, NT])
        has = sb("has", [P, NT])
        endf = sb("endf", [P, NT])
        end_i = sb("end_i", [P, NT], i32)
        rcnt = sb("rcnt", [P, NT])
        amp = sb("amp", [P, NT])
        dhi = sb("dhi", [P, 2, NT])
        dint = sb("dint", [P, 3, NT], i32)
        oh = sb("oh", [P, 2, P + NT])
        small = sb("small", [P, 16])
        fix_i = sb("fix_i", [P, 1], i32)
        pidx_i = sb("pidx_i", [P, 1], i32)
        fixr = sb("fixr", [P, SW])
        links = sb("links", [P, 2, P])
        linkb = sb("linkb", [P, 2, P])
        before = sb("before", [P, 2, P])
        carryT = sb("carryT", [P, 2, P])
        s1 = sb("s1", [P, 4, NT])
        stat = sb("stat", [P, 4, F])
        t1 = sb("t1", [P, 2, F])

        flat = states[:, :, :, :].rearrange("p a b c -> p (a b c)")
        dst_i = flat[:, 0:COLS].bitcast(i32)
        dst_f = flat[:, COLS:2 * COLS]
        same = flat[:, 2 * COLS:3 * COLS]
        fst = flat[0:1, 3 * COLS:3 * COLS + NCH].bitcast(i32)
        fstf = flat[0:1, 3 * COLS + NCH:3 * COLS + 2 * NCH]
        first_b = flat[:, 3 * COLS + 2 * NCH:3 * COLS + 3 * NCH]
        early = stage[:, :, :].rearrange("p a b -> p (a b)")
        wn = early[:, 0:4 * F].rearrange("p (a b) -> p a b", a=4)
        iorow = early[:, 4 * F:4 * F + P]
        iorow_i = early[:, 4 * F + P:4 * F + 2 * P].bitcast(i32)
        wT = tsb[0:F, :, :].rearrange("p a b -> p (a b)").rearrange("p (a b) -> p a b", a=4)
        diag2 = tsb[:, 0, :].rearrange("p (a b) -> p a b", a=2)
        zrow = fixr[0:1, :]
        gath = rows[:, 0:SLOTS * GC * F].rearrange("p (s c) -> p s c", s=SLOTS)
        chunks = rows[:, :].bitcast(i32).rearrange("p (s c) -> p s c", s=SLOTS)
        agg = rows[:, 0:SLOTS * SW].rearrange("p (s c) -> p s c", s=SLOTS)

        h_ps = ctx.enter_context(nc.psum_tensor("h_ps", [P, 4, 512], f32))
        t_ps = ctx.enter_context(nc.psum_tensor("t_ps", [P, 2, 512], f32))
        o_ps = ctx.enter_context(nc.psum_tensor("o_ps", [P, 2, 512], f32))

        dst_in, src_in, ea_in, x_loaded, w_in, fst_in = (sem(n) for n in (
            "dst_in", "src_in", "ea_in", "x_loaded", "w_in", "fst_in"))
        zero_in = sem("zero_in")
        act_step, dve_step, pool_step = sem("act_step"), sem("dve_step"), sem("pool_step")
        first_bc, first_ready, chrow_ready = sem("first_bc"), sem("first_ready"), sem("chrow_ready")
        cidx_ready, chunk_counted, le_done = sem("cidx_ready"), sem("chunk_counted"), sem("le_done")
        chunk_got = [sem(f"chunk_got{s}") for s in range(SLOTS)]
        masks_ready = sem("masks_ready")
        w_t, w_tc, w_p, w_pc = sem("w_t"), sem("w_tc"), sem("w_p"), sem("w_pc")
        ends_ready, starts_ps = sem("ends_ready"), sem("starts_ps")
        onehot_ready, onehot_used = sem("onehot_ready"), sem("onehot_used")
        link_in, link_ps, logs_ready, logsum_ps = sem("link_in"), sem("link_ps"), sem("logs_ready"), sem("logsum_ps")
        x_ready, pair_staged, pair_T, pair_Tc, pair_y, pair_yc = (sem(n) for n in (
            "x_ready", "pair_staged", "pair_T", "pair_Tc", "pair_y", "pair_yc"))
        y_stored = sem("y_stored")
        idx_staged, const_staged, ea_T, ea_Tc, h_ready, state_done = (sem(n) for n in (
            "idx_staged", "const_staged", "ea_T", "ea_Tc", "h_ready", "state_done"))
        got = [sem(f"got{s}") for s in range(SLOTS)]
        stored = [sem(f"stored{s}") for s in range(SLOTS)]
        tail_T, tail_used, carry_T, carry_back = sem("tail_T"), sem("tail_used"), sem("carry_T"), sem("carry_back")
        fix_got, fix_ready, fix_stored = sem("fix_got"), sem("fix_ready"), sem("fix_stored")
        nidx_staged, nx_staged, mean_ready, node_T, node_Tc, node_o, node_done = (sem(n) for n in (
            "nidx_staged", "nx_staged", "mean_ready", "node_T", "node_Tc", "node_o", "node_done"))
        agg_got = [sem(f"agg_got{s}") for s in range(SLOTS)]
        mean_ps, sq_in, sq_ready, var_ps, var_in, std_ready = (sem(n) for n in (
            "mean_ps", "sq_in", "sq_ready", "var_ps", "var_in", "std_ready"))
        turn = sem("turn")
        res_ready, res_stored = sem("res_ready"), sem("res_stored")

        def linker(eng, s):
            n = [0]

            def link(ins):
                n[0] += 1
                ins.then_inc(s, 1)
                eng.wait_ge(s, n[0])
            return link

        FULL = NG // SLOTS
        NFULL = NT // SLOTS

        def over_groups(eng, step):
            for s in range(SLOTS):
                step(0, s, False)
            with eng.Fori(1, FULL - 1) as i:
                for s in range(SLOTS):
                    step(i, s, False)
            for g in range((FULL - 1) * SLOTS, NG):
                step(g // SLOTS, g % SLOTS, True)

        def over_tiles(eng, step):
            for s in range(SLOTS):
                step(0, s)
            with eng.Fori(1, NFULL) as i:
                for s in range(SLOTS):
                    step(i, s)
            for t in range(NFULL * SLOTS, NT):
                step(t // SLOTS, t % SLOTS)

        def is0(i):
            return isinstance(i, int) and i == 0

        def uses(layer, s, total):
            return layer * len(range(s, total, SLOTS))

        PAIRS = NT // 2
        assert NT == 2 * PAIRS + 1 and NT == NFULL * SLOTS + 1 and NCH * CHUNK == E

        block = ctx.enter_context(nc.Block())

        @block.sync
        def _(sp):
            sp.dma_start(fst[0:1, :], dst.rearrange("(c k) -> k c", k=CHUNK)[0:1, :], allow_slow_non_contiguous=True).then_inc(fst_in, 16)
            sp.wait_ge(pool_step, 4)
            cut = 7 * 16
            whole = dst[0:(P - 1) * COLS].rearrange("(p c) -> p c", c=COLS)
            sp.dma_start(o_all[:, 0:NT - 1, :], x[0:(NT - 1) * P, :].rearrange("(t p) f -> p t f", p=P)).then_inc(x_loaded, 16)
            sp.dma_start(o_all[0:NL, NT - 1, :], x[(NT - 1) * P:N, :]).then_inc(x_loaded, 16)
            for tile, dram, s in ((dst_i, dst, dst_in), (src_all, src, src_in)):
                v = dram[0:(P - 1) * COLS].rearrange("(p c) -> p c", c=COLS)
                sp.dma_start(tile[0:cut, :], v[0:cut, :]).then_inc(s, 16)
                sp.dma_start(tile[cut:P - 1, :], v[cut:P - 1, :]).then_inc(s, 16)
                sp.dma_start(tile[P - 1:P, 0:LASTC], dram[(P - 1) * COLS:E].rearrange("(p c) -> p c", p=1)).then_inc(s, 16)
            for l in range(LAYERS):
                sp.dma_start(w64[:, l, 0, :], Wpre[l, F:2 * F, :]).then_inc(w_in, 16)
                sp.dma_start(w64[:, l, 1, :], Wlin[l, :, :]).then_inc(w_in, 16)
                sp.dma_start(we[:, l, :], We[l, :, :]).then_inc(w_in, 16)
                sp.dma_start(bd1[0:F, l, 0:F], Wpre[l, 0:F, :]).then_inc(w_in, 16)
                sp.dma_start(bd1[F:2 * F, l, F:2 * F], Wpre[l, 0:F, :]).then_inc(w_in, 16)
                sp.dma_start(bcol[:, l, 0:1], be[l, :].rearrange("(f o) -> f o", o=1), allow_slow_non_contiguous=True).then_inc(w_in, 16)
                sp.dma_start(bcol[:, l, 1:2], bpost[l, :].rearrange("(f o) -> f o", o=1), allow_slow_non_contiguous=True).then_inc(w_in, 16)
                for k, b in enumerate((bpre, blin, gamma, beta)):
                    sp.dma_start(brow[0:1, l, k, :], b[l:l + 1, :]).then_inc(w_in, 16)
            sp.wait_ge(dve_step, 1)
            for l in range(LAYERS):
                if l:
                    sp.wait_ge(w_t, 2 * l)
                for half, slot, part in ((0, 0, 3), (1, 0, 2), (0, 1, 6), (1, 1, 5), (0, 2, 1), (1, 2, 0), (0, 3, 4)):
                    sp.dma_start(wn[half * F:(half + 1) * F, slot, :],
                                 Wpost[l, part * F:(part + 1) * F, :]).then_inc(w_in, 16)
            body = ea[0:(P - 1) * COLS, :].rearrange("(p g c) k -> p g (c k)", g=NG, c=GC)
            quarter = -(-NG // 4)
            for g0 in range(0, NG, quarter):
                g1 = min(NG, g0 + quarter)
                sp.dma_start(comb[0:cut, g0:g1, 0:NEG], body[0:cut, g0:g1, :]).then_inc(ea_in, 16)
                sp.dma_start(comb[cut:P - 1, g0:g1, 0:NEG], body[cut:P - 1, g0:g1, :]).then_inc(ea_in, 16)
            lg, lc = LASTC // GC, LASTC % GC
            last = ea[(P - 1) * COLS:E, :]
            sp.dma_start(comb[P - 1:P, 0:lg, 0:NEG],
                         last[0:lg * GC, :].rearrange("(p g c) k -> p g (c k)", p=1, c=GC)).then_inc(ea_in, 16)
            if lc:
                sp.dma_start(comb[P - 1:P, lg, 0:lc * ED],
                             last[lg * GC:, :].rearrange("(p c) k -> p (c k)", p=1)).then_inc(ea_in, 16)
            sp.dma_start(st_dram[ZROW:ZROW + 1, :], zrow[0:1, :]).then_inc(zero_in, 16)

            st_v = st_dram[0:ZROW, :].rearrange("(p c) w -> p c w", c=COLS)
            for l in range(LAYERS):
                sp.wait_ge(pair_yc, (PAIRS + 1) * (l + 1))
                sp.dma_start(y_dram[0:(NT - 1) * P, :].rearrange("(t p) f -> p t f", p=P),
                             o_all[:, 0:NT - 1, :]).then_inc(y_stored, 16)
                sp.dma_start(y_dram[(NT - 1) * P:N, :], o_all[0:NL, NT - 1, :]).then_inc(y_stored, 16)

                def store(i, s, near_end):
                    sp.wait_ge(state_done, 3 * GC * (NG * l + s + 1) + 3 * GC * SLOTS * i)
                    c0 = GC * SLOTS * i + GC * s
                    sp.dma_start(st_v[:, bass.ds(c0, GC), :], states[:, s, :, :]).then_inc(stored[s], 16)
                over_groups(sp, store)
            sp.wait_ge(var_ps, LAYERS)
            sp.dma_start(x_all[:, 0:NT - 1, :], x[0:(NT - 1) * P, :].rearrange("(t p) f -> p t f", p=P)).then_inc(x_loaded, 16)
            sp.dma_start(x_all[0:NL, NT - 1, :], x[(NT - 1) * P:N, :]).then_inc(x_loaded, 16)
            sp.wait_ge(res_ready, 1)
            sp.dma_start(out[0:(NT - 1) * P, :].rearrange("(t p) f -> p t f", p=P), o_all[:, 0:NT - 1, :]).then_inc(res_stored, 16)
            sp.dma_start(out[(NT - 1) * P:N, :], o_all[0:NL, NT - 1, :]).then_inc(res_stored, 16)
            sp.wait_ge(res_stored, 32)
            sp.wait_ge(zero_in, 16)
            for s in range(SLOTS):
                sp.wait_ge(stored[s], 16 * uses(LAYERS, s, NG))
            sp.wait_ge(fix_stored, 16 * LAYERS)

        @block.gpsimd
        def _(pool):
            lg = LASTC // GC
            link = linker(pool, pool_step)
            link(pool.memset(dst_i[96:P, LASTC:COLS], 8191))
            link(pool.memset(src_all[96:P, LASTC:COLS], 0))
            link(pool.memset(o_all[96:P, NT - 1, :], 0.0))
            link(pool.memset(bd1[:, :, :], 0.0))
            link(pool.iota(nidi[:, :], pattern=[[P, NT]], base=0, channel_multiplier=1))
            link(pool.iota(iorow_i[:, :], pattern=[[1, P]], base=0, channel_multiplier=0))
            link(pool.iota(pidx_i[:, :], pattern=[[0, 1]], base=0, channel_multiplier=1))
            link(pool.memset(ident[:, :], 0.0))
            link(pool.memset(shiftm[:, :], 0.0))
            link(pool.memset(wrapm[:, :], 0.0))
            link(pool.memset(bdmask[:, :], 1.0))
            link(pool.affine_select(out=ident[:, :], in_=ident[:, :], compare_op=ALU.not_equal, fill=1.0,
                               base=0, pattern=[[-1, P]], channel_multiplier=1))
            link(pool.affine_select(out=shiftm[:, :], in_=shiftm[:, :], compare_op=ALU.not_equal, fill=1.0,
                               base=-1, pattern=[[1, P]], channel_multiplier=-1))
            link(pool.affine_select(out=wrapm[:, :], in_=wrapm[:, :], compare_op=ALU.not_equal, fill=1.0,
                               base=1 - P, pattern=[[-1, P]], channel_multiplier=1))
            link(pool.affine_select(out=bdmask[:, :], in_=bdmask[:, :], compare_op=ALU.is_ge, fill=0.0,
                               base=0, pattern=[[-ED, GC]], channel_multiplier=1))
            link(pool.affine_select(out=bdmask[:, :], in_=bdmask[:, :], compare_op=ALU.is_ge, fill=0.0,
                               base=ED - 1, pattern=[[ED, GC]], channel_multiplier=-1))

            dst_ch = dst.rearrange("(c k) -> c k", k=CHUNK)

            def chunk(i, s):
                pool.wait_ge(cidx_ready, SLOTS * i + s + 1)
                if not is0(i):
                    pool.wait_ge(chunk_counted, SLOTS * (i - 1) + s + 1)
                pool.sem_inc(turn, 1)
                pool.indirect_dma_start(chunks[:, s, :], None, dst_ch,
                                        bass.IndirectOffsetOnAxis(ap=idx[:, s, 0:1], axis=0)).then_inc(chunk_got[s], 16)
            over_tiles(pool, chunk)

            for l in range(LAYERS):
                pool.wait_ge(y_stored, 32 * (l + 1))
                if l == 0:
                    pool.wait_ge(chunk_counted, NT)
                else:
                    pool.wait_ge(node_T, 2 * NT * l)
                    pool.wait_ge(mean_ready, NT * l)

                def gather(i, s, near_end):
                    pool.wait_ge(idx_staged, NG * l + s + 1 + SLOTS * i)
                    if not is0(i):
                        pool.wait_ge(h_ready, NG * l + s + 1 + SLOTS * (i - 1))
                    pool.sem_inc(turn, 1)
                    for c in range(GC):
                        pool.indirect_dma_start(gath[:, s, c * F:(c + 1) * F], None, y_dram,
                                                bass.IndirectOffsetOnAxis(ap=idx[:, s, c:c + 1], axis=0)).then_inc(got[s], 16)
                over_groups(pool, gather)

                for s in range(SLOTS):
                    pool.wait_ge(stored[s], 16 * uses(l + 1, s, NG))
                pool.wait_ge(zero_in, 16)
                pool.indirect_dma_start(fixr[:, :], None, st_dram,
                                        bass.IndirectOffsetOnAxis(ap=fix_i[:, 0:1], axis=0)).then_inc(fix_got, 16)
                pool.wait_ge(fix_ready, l + 1)
                pool.indirect_dma_start(st_dram, bass.IndirectOffsetOnAxis(ap=fix_i[:, 0:1], axis=0),
                                        fixr[:, :], None).then_inc(fix_stored, 16)
                pool.wait_ge(fix_stored, 16 * (l + 1))
                pool.wait_ge(h_ready, NG * (l + 1))

                def node_rows(i, s):
                    pool.wait_ge(nidx_staged, NT * l + s + 1 + SLOTS * i)
                    if not is0(i):
                        pool.wait_ge(node_T, 2 * (NT * l + s + 1) + 2 * SLOTS * (i - 1))
                        pool.wait_ge(mean_ready, NT * l + s + 1 + SLOTS * (i - 1))
                    pool.sem_inc(turn, 1)
                    pool.indirect_dma_start(agg[:, s, :], None, st_dram,
                                            bass.IndirectOffsetOnAxis(ap=idx[:, s, 0:1], axis=0)).then_inc(agg_got[s], 16)
                over_tiles(pool, node_rows)

        @block.scalar
        def _(act):
            link = linker(act, act_step)

            def stage_chunk(i, s):
                act.copy(idx[:, s, 0:1], chrow_i[:, bass.ds(SLOTS * i + s, 1)]).then_inc(cidx_ready, 1)

            def count(i, s):
                act.wait_ge(chunk_got[s], 16 * i + 16)
                t = SLOTS * i + s
                act.activation(chunks[:, s, :].bitcast(f32), chunks[:, s, :], ACT.Sign, bias=nidh[:, bass.ds(t, 1)],
                               scale=-1.0, accum_out=sg[:, bass.ds(t, 1)]).then_inc(chunk_counted, 1)
            act.wait_ge(chrow_ready, 1)
            for s in range(SLOTS):
                stage_chunk(0, s)
            for s in range(SLOTS):
                count(0, s)
                stage_chunk(1, s)
            with act.Fori(1, NFULL - 1) as i:
                for s in range(SLOTS):
                    count(i, s)
                    stage_chunk(i + 1, s)
            for s in range(SLOTS):
                count(NFULL - 1, s)
                if NFULL * SLOTS + s < NT:
                    stage_chunk(NFULL, s)
            for s in range(NT - NFULL * SLOTS):
                count(NFULL, s)

            def project(l):
                act.wait_ge(x_ready, l + 1)

                def put(i, s):
                    act.copy(xp[:, s, :], x_all[:, bass.ds(4 * i + 2 * s, 2), :]).then_inc(pair_staged, 1)

                def take(i, s):
                    n = (PAIRS + 1) * l + s + 2 * i
                    act.wait_ge(pair_T, n + 1)
                    if n_pos(i, l):
                        act.wait_ge(pair_y, (n - 1))
                    act.copy(tsb[:, s, 0:P], t_ps[:, s, 0:P]).then_inc(pair_Tc, 1)
                put(0, 0)
                put(0, 1)
                for s in range(2):
                    take(0, s)
                    put(1, s)
                with act.Fori(1, PAIRS // 2 - 1) as i:
                    for s in range(2):
                        take(i, s)
                        put(i + 1, s)
                for s in range(2):
                    take(PAIRS // 2 - 1, s)
                    if s == 0:
                        act.copy(xp[:, 0, 0:F], x_all[:, NT - 1, :]).then_inc(pair_staged, 1)
                n = (PAIRS + 1) * l + PAIRS
                act.wait_ge(pair_T, n + 1)
                act.wait_ge(pair_y, n - 1)
                act.copy(tsb[0:F, 0, 0:P], t_ps[0:F, 0, 0:P]).then_inc(pair_Tc, 1)

            def n_pos(i, l):
                return l > 0 or not is0(i)

            def edges(l):
                def stage_idx(i, s):
                    act.copy(idx[:, s, :], src_all[:, bass.ds(GC * SLOTS * i + GC * s, GC)]).then_inc(idx_staged, 1)

                def stage_const(i, s):
                    g = bass.ds(SLOTS * i + s, 1)
                    act.copy(stage[:, s, 0:NEG + GC], comb[:, g, :].rearrange("p o c -> p (o c)"))
                    act.activation(stage[:, s, NEG + GC:CW], comb[:, g, NEG:NEG + GC].rearrange("p o c -> p (o c)"),
                                   ACT.Copy, bias=-BIG, scale=BIG).then_inc(const_staged, 1)

                def take(i, s):
                    n = NG * l + s + SLOTS * i
                    act.wait_ge(ea_T, n + 1)
                    if l > 0 or not is0(i) or s >= 2:
                        act.wait_ge(h_ready, n - 1)
                    act.copy(eaT[:, s % 2, :], t_ps[:, s % 2, 0:P]).then_inc(ea_Tc, 1)
                for s in range(SLOTS):
                    stage_idx(0, s)
                    stage_const(0, s)
                take(0, 0)

                def step(i, s, near_end):
                    g = SLOTS * i + s if isinstance(i, int) else None
                    if g is None or g + 1 < NG:
                        take(i + (s + 1) // SLOTS, (s + 1) % SLOTS)
                    if g is None or g + SLOTS < NG:
                        act.wait_ge(got[s], 16 * GC * (uses(l, s, NG) + 1) + 16 * GC * i)
                        stage_idx(i + 1, s)
                        act.wait_ge(state_done, 3 * GC * (NG * l + s + 1) + 3 * GC * SLOTS * i)
                        stage_const(i + 1, s)
                over_groups(act, step)

            def nodes(l):
                def stage_idx(i, s):
                    act.copy(idx[:, s, 0:1], end_i[:, bass.ds(SLOTS * i + s, 1)]).then_inc(nidx_staged, 1)

                def stage_x(i, s):
                    act.copy(xp[:, s, F:2 * F], x_all[:, bass.ds(SLOTS * i + s, 1), :].rearrange("p o c -> p (o c)")).then_inc(nx_staged, 1)

                def take(i, s):
                    n = NT * l + s + SLOTS * i
                    act.wait_ge(node_T, 2 * n + 2)
                    if l > 0 or not is0(i) or s >= 2:
                        act.wait_ge(node_o, n - 1)
                    act.copy(tsb[:, s % 2, :], t_ps[:, s % 2, 0:2 * P]).then_inc(node_Tc, 1)
                for s in range(SLOTS):
                    act.wait_ge(got[s], 16 * GC * uses(l + 1, s, NG))
                    stage_idx(0, s)
                    stage_x(0, s)

                def step(i, s):
                    take(i, s)
                    t = SLOTS * i + s if isinstance(i, int) else None
                    if t is None or t + SLOTS < NT:
                        stage_idx(i + 1, s)
                        stage_x(i + 1, s)
                for s in range(SLOTS):
                    step(0, s)
                with act.Fori(1, NFULL - 1) as i:
                    for s in range(SLOTS):
                        step(i, s)
                for t in range((NFULL - 1) * SLOTS, NT):
                    step(t // SLOTS, t % SLOTS)

            def norm(l):
                act.wait_ge(sq_in, l + 2)
                act.activation(x_all[:, :, :], o_all[:, :, :], ACT.Square).then_inc(sq_ready, 1)
                act.wait_ge(var_in, l + 2)
                act.activation(stat[:, 2, :], stat[:, 1, :], ACT.Sqrt).then_inc(std_ready, 1)

            act.wait_ge(sq_in, 1)
            act.activation(o_all[:, :, :], x_all[:, :, :], ACT.Square).then_inc(sq_ready, 1)
            act.wait_ge(var_in, 1)
            act.activation(s1[:, 2, :], s1[:, 1, :], ACT.Sqrt).then_inc(std_ready, 1)

            project(0)
            act.wait_ge(onehot_used, NT)
            act.activation(small[0:P, 8:8 + 1], o_ps[:, 0, NT - 1:NT], ACT.Ln, bias=1.0).then_inc(act_step, 1)
            act.activation(dhi[:, 0, 0:NT - 1], o_ps[:, 0, 0:NT - 1], ACT.Ln, bias=1.0, accum_out=small[:, 9:10]).then_inc(logs_ready, 1)
            act.activation(amp[:, :], cnt[:, :], ACT.Ln, bias=1.0).then_inc(logs_ready, 1)
            act.wait_ge(masks_ready, 1)
            act.wait_ge(src_in, 48)
            act.wait_ge(ea_in, 16 * (8 + 1 + (1 if LASTC % GC else 0)))
            for l in range(LAYERS):
                edges(l)
                nodes(l)
                norm(l)
                if l + 1 < LAYERS:
                    project(l + 1)

        @block.vector
        def _(dve):
            link = linker(dve, dve_step)

            def wide(ap):
                return ap.unsqueeze(2).broadcast_to([P, NT, F])

            def over_nodes(ap):
                return ap.unsqueeze(1).broadcast_to([P, NT, F])

            dve.memset(ones[:, :], 1.0).then_inc(first_bc, 1)
            dve.memset(zrow[:, :], 0.0)
            dve.memset(wn[:, 3, :], 0.0)
            link(dve.memset(comb[96:P, LASTC // GC:NG, 0:NEG], 0.0))
            dve.wait_ge(fst_in, 16)
            dve.tensor_copy(fstf[0:1, :], fst[0:1, :]).then_inc(first_bc, 1)
            dve.wait_ge(pool_step, 16)
            link(dve.tensor_copy(nid[:, :], nidi[:, :]))
            dve.tensor_scalar(nidh[:, :], nid[:, :], 0.5, None, ALU.add)
            link(dve.tensor_copy(iorow[:, :], iorow_i[:, :]))
            dve.wait_ge(first_ready, 1)
            link(dve.tensor_copy(first_b[:, :], o_ps[:, 0, 0:NCH]))

            def le_step(i, s):
                t = SLOTS * i + s
                if s >= 2 or not is0(i):
                    dve.wait_ge(le_done, t - 1)
                dve.tensor_scalar(o_ps[:, s % 2, 0:NCH], first_b[:, :], nid[:, bass.ds(t, 1)], None,
                                  ALU.is_le, ALU.add, accum_out=le[:, bass.ds(t, 1)]).then_inc(le_done, 1)
            over_tiles(dve, le_step)
            dve.wait_ge(le_done, NT)
            link(dve.tensor_scalar(chrow[:, :], le[:, :], -1.0, 0.0, ALU.add, ALU.max))
            dve.tensor_copy(chrow_i[:, :], chrow[:, :]).then_inc(chrow_ready, 1)

            dve.wait_ge(x_loaded, 32)
            link(dve.tensor_reduce(s1[:, 0, :], o_all[:, :, :], AX.X, ALU.add))
            link(dve.tensor_scalar(s1[:, 0, :], s1[:, 0, :], 1.0 / F, None, ALU.mult))
            dve.tensor_tensor(x_all[:, :, :], o_all[:, :, :], wide(s1[:, 0, :]), ALU.subtract).then_inc(sq_in, 1)
            dve.wait_ge(sq_ready, 1)
            link(dve.tensor_reduce(s1[:, 1, :], o_all[:, :, :], AX.X, ALU.add))
            dve.tensor_scalar(s1[:, 1, :], s1[:, 1, :], 1.0 / F, EPS, ALU.mult, ALU.add).then_inc(var_in, 1)
            dve.wait_ge(std_ready, 1)
            link(dve.reciprocal(s1[:, 3, :], s1[:, 2, :]))
            link(dve.tensor_tensor(x_all[:, :, :], x_all[:, :, :], wide(s1[:, 3, :]), ALU.mult))
            dve.tensor_scalar(x_all[:, :, :], x_all[:, :, :], 0.0, None, ALU.max).then_inc(x_ready, 1)

            for l in range(LAYERS):
                dve.wait_ge(w_t, 2 * l + 1)
                dve.tensor_copy(weT[:, :, :], h_ps[0:F, 0, 0:ED].unsqueeze(1).broadcast_to([F, GC, ED])).then_inc(w_tc, 1)
                dve.wait_ge(w_t, 2 * l + 2)
                dve.tensor_copy(wT[:, :, :], h_ps[0:F, 1, :].rearrange("p (a b) -> p a b", a=4)).then_inc(w_tc, 1)
                dve.wait_ge(w_p, 4 * l + 4)
                dve.tensor_tensor(bd[:, l, :].rearrange("p (j f) -> p j f", j=GC),
                                  h_ps[:, 2, 0:F].unsqueeze(1).broadcast_to([P, GC, F]),
                                  bdmask[:, :].unsqueeze(2).broadcast_to([P, GC, F]), ALU.mult)
                dve.tensor_copy(rw[:, l, :, :], h_ps[:, 3, 0:4 * F].rearrange("p (a b) -> p a b", a=4))
                dve.tensor_copy(crow[0:1, l, :, :], h_ps[0:1, 2, F:4 * F].rearrange("p (a b) -> p a b", a=3))
                dve.tensor_copy(gb[:, l, :, :], h_ps[:, 3, 4 * F:6 * F].rearrange("p (a b) -> p a b", a=2)).then_inc(w_pc, 1)

            def project(l):
                def take(i, s):
                    dve.wait_ge(pair_y, (PAIRS + 1) * l + s + 1 + 2 * i)
                    dve.tensor_copy(o_all[:, bass.ds(4 * i + 2 * s, 2), :],
                                    o_ps[:, s, 0:2 * F].rearrange("p (a b) -> p a b", a=2)).then_inc(pair_yc, 1)
                for s in range(2):
                    take(0, s)
                with dve.Fori(1, PAIRS // 2) as i:
                    for s in range(2):
                        take(i, s)
                dve.wait_ge(pair_y, (PAIRS + 1) * (l + 1))
                dve.tensor_copy(o_all[:, NT - 1, :], o_ps[:, 0, 0:F]).then_inc(pair_yc, 1)
            project(0)

            dve.wait_ge(dst_in, 48)
            link(dve.tensor_copy(dst_f[:, :], dst_i[:, :]))
            dve.memset(same[:, 0:1], 0.0)
            link(dve.tensor_tensor(same[:, 1:COLS], dst_f[:, 1:COLS], dst_f[:, 0:COLS - 1], ALU.is_equal))
            same_g = same.rearrange("p (g c) -> p g c", c=GC)
            dve.tensor_copy(comb[:, :, NEG:NEG + GC], same_g)
            dve.tensor_copy(small[:, 0:1], dst_f[:, 0:1])
            link(dve.tensor_copy(small[:, 1:2], dst_f[:, COLS - 1:COLS]))
            link(dve.tensor_scalar(same, dst_f, small[:, 0:1], None, ALU.is_equal, ALU.add, accum_out=small[:, 2:3]))
            link(dve.tensor_copy(small[:, 3:4], pidx_i[:, 0:1]))
            dve.tensor_scalar(small[:, 4:5], small[:, 3:4], float(COLS), -1.0, ALU.mult, ALU.add)
            link(dve.tensor_scalar(small[:, 12:13], small[:, 3:4], 1.0, None, ALU.min))
            link(dve.tensor_tensor(small[:, 5:6], small[:, 4:5], small[:, 2:3], ALU.add))
            link(dve.tensor_copy(fix_i[:, :], small[:, 5:6]))
            dve.memset(states[:, SLOTS - 1, GC - 1, :], 0.0).then_inc(link_in, 1)
            dve.wait_ge(link_ps, 1)
            link(dve.tensor_copy(small[:, 6:8], o_ps[:, 1, 0:2]))
            dve.tensor_tensor(small[:, 10:11], small[:, 7:8], small[:, 0:1], ALU.is_equal)
            link(dve.tensor_tensor(small[:, 11:12], small[:, 7:8], small[:, 6:7], ALU.is_equal))
            link(dve.tensor_tensor(small[:, 10:11], small[:, 10:11], small[:, 12:13], ALU.mult))
            link(dve.tensor_tensor(small[:, 11:12], small[:, 10:11], small[:, 11:12], ALU.mult))
            dve.tensor_scalar(diag2[:, 0, :], ident[:, :], small[:, 10:11], None, ALU.mult)
            dve.tensor_scalar(diag2[:, 1, :], ident[:, :], small[:, 11:12], None, ALU.mult).then_inc(link_in, 1)
            dve.wait_ge(link_ps, 2)
            link(dve.tensor_copy(links[:, :, :], o_ps[:, 1, 0:2 * P].rearrange("p (a b) -> p a b", a=2)))
            dve.tensor_scalar(linkb[0:F, :, :], links[0:F, :, :], -1.0, BIG, ALU.add, ALU.mult)
            dve.tensor_scalar(linkb[F:P, :, :], links[F:P, :, :], -1.0, -BIG, ALU.add, ALU.mult)
            dve.memset(before[0:F, 0, 0:1], -BIG)
            dve.memset(before[F:P, 0, 0:1], BIG)
            link(dve.memset(before[0:F, 1, 0:1], 0.0))

            dve.wait_ge(chunk_counted, NT)
            link(dve.tensor_scalar(ends[:, :], sg[:, :], float(CHUNK), 0.5, ALU.add, ALU.mult))
            link(dve.tensor_scalar(chrow[:, :], chrow[:, :], float(CHUNK), None, ALU.mult))
            dve.tensor_tensor(ends[:, :], ends[:, :], chrow[:, :], ALU.add).then_inc(ends_ready, 1)
            dve.wait_ge(starts_ps, 1)
            link(dve.tensor_tensor(deg[:, :], ends[:, :], o_ps[:, 1, 0:NT], ALU.subtract))
            dve.tensor_scalar(has[:, :], deg[:, :], 1.0, None, ALU.min)
            dve.tensor_scalar(cnt[:, :], deg[:, :], 1.0, None, ALU.max)
            link(dve.tensor_scalar(endf[:, :], ends[:, :], -1.0 - ZROW, None, ALU.add))
            link(dve.reciprocal(rcnt[:, :], cnt[:, :]))
            link(dve.tensor_tensor(endf[:, :], endf[:, :], has[:, :], ALU.mult))
            link(dve.tensor_scalar(endf[:, :], endf[:, :], float(ZROW), None, ALU.add))
            link(dve.tensor_copy(end_i[:, :], endf[:, :]))
            link(dve.tensor_copy(dint[:, 0, :], deg[:, :]))
            dve.tensor_scalar(dint[:, 1, :], dint[:, 0, :], 7, None, ALU.logical_shift_right)
            link(dve.tensor_scalar(dint[:, 2, :], dint[:, 0, :], P - 1, None, ALU.bitwise_and))
            link(dve.tensor_copy(dhi[:, :, :], dint[:, 1:3, :]))

            def one_hot(i, s):
                t = SLOTS * i + s
                if s >= 2 or not is0(i):
                    dve.wait_ge(onehot_used, t - 1)
                dve.tensor_scalar(oh[:, s % 2, 0:P], iorow[:, :], dhi[:, 1, bass.ds(t, 1)], None, ALU.is_equal)
                dve.tensor_scalar(oh[:, s % 2, P:P + NT], iorow[:, 0:NT], dhi[:, 0, bass.ds(t, 1)], None, ALU.is_equal).then_inc(onehot_ready, 1)
            over_tiles(dve, one_hot)
            dve.wait_ge(logs_ready, 2)
            dve.wait_ge(logsum_ps, 1)
            link(dve.tensor_reduce(small[:, 13:14], o_ps[:, 1, 0:2], AX.X, ALU.add))
            link(dve.tensor_scalar(small[:, 14:15], small[:, 13:14], 1.0 / N, None, ALU.mult))
            link(dve.reciprocal(small[:, 15:16], small[:, 14:15]))
            dve.tensor_scalar(amp[:, :], amp[:, :], small[:, 15:16], None, ALU.mult).then_inc(masks_ready, 1)

            def edges(l):
                def step(i, s, near_end):
                    dve.wait_ge(h_ready, NG * l + s + 1 + SLOTS * i)
                    if l > 0 or not is0(i):
                        dve.wait_ge(stored[s], 16 * uses(l, s, NG) + 16 * i)
                    for c in range(GC):
                        n = 3 * (COLS * l + GC * s + c)
                        if l > 0 or not is0(i) or s or c:
                            dve.wait_ge(state_done, n + 3 * GC * SLOTS * i)
                        last = states[:, s, c - 1, :] if c else states[:, (s - 1) % SLOTS, GC - 1, :]
                        h = h_ps[:, s, c * F:(c + 1) * F]
                        one = stage[:, s, NEG + c:NEG + c + 1]
                        neg = stage[:, s, NEG + GC + c:NEG + GC + c + 1]
                        for k, (mask, op0, op1) in enumerate(((neg, ALU.add, ALU.max), (neg, ALU.subtract, ALU.min),
                                                              (one, ALU.mult, ALU.add))):
                            dve.scalar_tensor_tensor(out=states[:, s, c, k * F:(k + 1) * F], in0=last[:, k * F:(k + 1) * F],
                                                     scalar=mask, in1=h, op0=op0, op1=op1).then_inc(state_done, 1)
                over_groups(dve, step)

                dve.wait_ge(tail_T, 2 * l + 2)
                dve.tensor_tensor(before[:, 0, 1:P], t_ps[:, 0, 0:P - 1], linkb[:, 0, 1:P], ALU.add)
                link(dve.tensor_tensor(before[0:F, 1, 1:P], t_ps[0:F, 0, P:2 * P - 1], links[0:F, 0, 1:P], ALU.mult))
                dve.tensor_tensor_scan(carryT[0:F, 0, :], linkb[0:F, 1, :], before[0:F, 0, :], -BIG, ALU.add, ALU.max)
                dve.tensor_tensor_scan(carryT[F:P, 0, :], linkb[F:P, 1, :], before[F:P, 0, :], BIG, ALU.add, ALU.min)
                dve.tensor_tensor_scan(carryT[0:F, 1, :], links[0:F, 1, :], before[0:F, 1, :], 0.0, ALU.mult, ALU.add).then_inc(carry_T, 1)
                dve.wait_ge(carry_back, 2 * l + 2)
                dve.wait_ge(fix_got, 16 * (l + 1))
                dve.tensor_tensor(fixr[:, 0:F], fixr[:, 0:F], t_ps[:, 1, 0:F], ALU.max)
                dve.tensor_tensor(fixr[:, F:2 * F], fixr[:, F:2 * F], t_ps[:, 1, F:2 * F], ALU.min)
                dve.tensor_tensor(fixr[:, 2 * F:SW], fixr[:, 2 * F:SW], t_ps[:, 1, 2 * F:SW], ALU.add).then_inc(fix_ready, 1)

            def nodes(l):
                def mean(i, s):
                    dve.wait_ge(agg_got[s], 16 * uses(l, s, NT) + 16 + 16 * i)
                    if l > 0 or not is0(i):
                        dve.wait_ge(node_T, 2 * (NT * l + s + 1) + 2 * SLOTS * (i - 1))
                    dve.tensor_scalar(xp[:, s, 0:F], agg[:, s, 2 * F:SW], rcnt[:, bass.ds(SLOTS * i + s, 1)], None, ALU.mult).then_inc(mean_ready, 1)

                def output(i, s):
                    n = NT * l + s + SLOTS * i
                    t = SLOTS * i + s
                    dve.wait_ge(node_o, n + 1)
                    dve.tensor_scalar(t1[:, s % 2, :], o_ps[:, s % 2, F:2 * F], amp[:, bass.ds(t, 1)], None, ALU.mult).then_inc(node_done, 1)
                    dve.wait_ge(node_done, 2 * n + 1)
                    dve.tensor_tensor(o_all[:, bass.ds(t, 1), :].rearrange("p o c -> p (o c)"), o_ps[:, s % 2, 0:F], t1[:, s % 2, :], ALU.add).then_inc(node_done, 1)

                def step(i, s):
                    mean(i, s)
                    output(i, s)
                over_tiles(dve, step)

            def norm(l, last):
                dve.wait_ge(mean_ps, l + 1)
                dve.wait_ge(node_done, 2 * NT * (l + 1))
                link(dve.tensor_reduce(stat[:, 0, :], h_ps[:, 0, :].rearrange("p (a f) -> p f a", f=F), AX.X, ALU.add))
                link(dve.tensor_scalar(stat[:, 0, :], stat[:, 0, :], 1.0 / N, None, ALU.mult))
                dve.tensor_tensor(o_all[:, :, :], o_all[:, :, :], over_nodes(stat[:, 0, :]), ALU.subtract).then_inc(sq_in, 1)
                dve.wait_ge(var_ps, l + 1)
                link(dve.tensor_reduce(stat[:, 1, :], h_ps[:, 1, :].rearrange("p (a f) -> p f a", f=F), AX.X, ALU.add))
                dve.tensor_scalar(stat[:, 1, :], stat[:, 1, :], 1.0 / N, EPS, ALU.mult, ALU.add).then_inc(var_in, 1)
                dve.wait_ge(std_ready, l + 2)
                link(dve.reciprocal(stat[:, 3, :], stat[:, 2, :]))
                link(dve.tensor_tensor(stat[:, 3, :], stat[:, 3, :], gb[:, l, 0, :], ALU.mult))
                link(dve.tensor_tensor(o_all[:, :, :], o_all[:, :, :], over_nodes(stat[:, 3, :]), ALU.mult))
                link(dve.tensor_tensor(o_all[:, :, :], o_all[:, :, :], over_nodes(gb[:, l, 1, :]), ALU.add))
                if last:
                    dve.wait_ge(x_loaded, 64)
                    dve.scalar_tensor_tensor(out=o_all[:, :, :], in0=o_all[:, :, :], scalar=0.0, in1=x_all[:, :, :],
                                             op0=ALU.max, op1=ALU.add).then_inc(res_ready, 1)
                else:
                    dve.tensor_scalar(x_all[:, :, :], o_all[:, :, :], 0.0, None, ALU.max).then_inc(x_ready, 1)

            for l in range(LAYERS):
                edges(l)
                nodes(l)
                norm(l, l + 1 == LAYERS)
                if l + 1 < LAYERS:
                    project(l + 1)

        @block.tensor
        def _(pe):
            pe.wait_ge(first_bc, 2)
            pe.matmul(o_ps[:, 0, 0:NCH], ones[0:1, :], fstf[0:1, :], start=True, stop=True).then_inc(first_ready, 1)

            pe.wait_ge(pool_step, 16)
            shared, wide_rows = 11 * LAYERS, 7
            pe.wait_ge(dve_step, 1)
            for l in range(LAYERS):
                pe.wait_ge(w_in, 16 * (shared + wide_rows * (l + 1)))
                if l:
                    pe.wait_ge(w_pc, l)
                pe.transpose(h_ps[0:F, 0, 0:ED], we[:, l, :], ident[0:ED, 0:ED]).then_inc(w_t, 1)
                for k in range(4):
                    t = pe.transpose(h_ps[0:F, 1, k * P:(k + 1) * P], wn[:, k, :], ident[:, :])
                t.then_inc(w_t, 1)
                pe.wait_ge(w_tc, 2 * l + 2)
                pe.matmul(h_ps[:, 2, 0:F], weT[:, :, :].rearrange("p a b -> p (a b)"), w64[:, l, 0, :], start=True, stop=True).then_inc(w_p, 1)
                for k in range(4):
                    m = pe.matmul(h_ps[:, 3, k * F:(k + 1) * F], wT[:, k, :], w64[:, l, 1, :], start=True, stop=True)
                m.then_inc(w_p, 1)
                for k, (col, w, row) in enumerate(((0, 0, 0), (0, 0, 0), (1, 1, 1))):
                    dstc = h_ps[0:1, 2, (k + 1) * F:(k + 2) * F]
                    pe.matmul(dstc, bcol[:, l, col:col + 1], w64[:, l, w, :], start=True, stop=False)
                    m = pe.matmul(dstc, ones[0:1, 0:1], brow[0:1, l, row, :], start=False, stop=True)
                m.then_inc(w_p, 1)
                pe.matmul(h_ps[:, 3, 4 * F:6 * F], ones[0:1, :], brow[0:1, l, 2:4, :].rearrange("p a b -> p (a b)"), start=True, stop=True).then_inc(w_p, 1)

            def project(l):
                def step(i, s):
                    n = (PAIRS + 1) * l + s + 2 * i
                    pe.wait_ge(pair_staged, n + 1)
                    if not is0(i) or l:
                        pe.wait_ge(pair_Tc, n - 1)
                    pe.transpose(t_ps[:, s, 0:P], xp[:, s, :], ident[:, :]).then_inc(pair_T, 1)
                    pe.wait_ge(pair_Tc, n + 1)
                    if not is0(i) or l:
                        pe.wait_ge(pair_yc, n - 1)
                    pe.matmul(o_ps[:, s, 0:2 * F], tsb[:, s, 0:P], bd1[:, l, :], start=True, stop=False)
                    pe.matmul(o_ps[:, s, 0:2 * F], ones[0:1, :], crow[0:1, l, 0:2, :].rearrange("p a b -> p (a b)"),
                              start=False, stop=True).then_inc(pair_y, 1)
                for s in range(2):
                    step(0, s)
                with pe.Fori(1, PAIRS // 2) as i:
                    for s in range(2):
                        step(i, s)
                n = (PAIRS + 1) * l + PAIRS
                pe.wait_ge(pair_staged, n + 1)
                pe.wait_ge(pair_Tc, n - 1)
                pe.transpose(t_ps[0:F, 0, 0:P], xp[:, 0, 0:F], ident[:, :]).then_inc(pair_T, 1)
                pe.wait_ge(pair_Tc, n + 1)
                pe.wait_ge(pair_yc, n - 1)
                pe.matmul(o_ps[:, 0, 0:F], tsb[0:F, 0, 0:P], bd1[0:F, l, 0:F], start=True, stop=False)
                pe.matmul(o_ps[:, 0, 0:F], ones[0:1, :], crow[0:1, l, 0, :], start=False, stop=True).then_inc(pair_y, 1)

            pe.wait_ge(w_pc, LAYERS)
            pe.wait_ge(chrow_ready, 1)
            project(0)

            pe.wait_ge(pair_yc, PAIRS + 1)
            pe.wait_ge(link_in, 1)
            pe.matmul(o_ps[:, 1, 0:2], shiftm[:, :], small[:, 0:2], start=True, stop=True).then_inc(link_ps, 1)
            pe.wait_ge(link_in, 2)
            pe.matmul(o_ps[:, 1, 0:2 * P], ones[:, :], diag2[:, :, :].rearrange("p a b -> p (a b)"), start=True, stop=True).then_inc(link_ps, 1)
            pe.wait_ge(ends_ready, 1)
            pe.matmul(o_ps[:, 1, 0:NT], shiftm[:, :], ends[:, :], start=True, stop=False)
            pe.matmul(o_ps[:, 1, 1:NT], wrapm[:, :], ends[:, 0:NT - 1], start=False, stop=True).then_inc(starts_ps, 1)

            def hist(i, s):
                t = SLOTS * i + s
                pe.wait_ge(onehot_ready, t + 1)
                k = NL if isinstance(i, int) and t == NT - 1 else P
                last = isinstance(i, int) and t == NT - 1
                m = pe.matmul(o_ps[:, 0, 0:NT], oh[0:k, s % 2, 0:P], oh[0:k, s % 2, P:P + NT], start=isinstance(i, int) and t == 0, stop=last)
                m.then_inc(onehot_used, 1)
            over_tiles(pe, hist)
            pe.wait_ge(logs_ready, 2)
            pe.wait_ge(act_step, 1)
            pe.matmul(o_ps[:, 1, 0:1], ones[0:NL, :], small[0:NL, 8:9], start=True, stop=True)
            pe.matmul(o_ps[:, 1, 1:2], ones[:, :], small[:, 9:10], start=True, stop=True).then_inc(logsum_ps, 1)

            def edges(l):
                def turn(i, s):
                    n = NG * l + s + SLOTS * i
                    pe.wait_ge(const_staged, n + 1)
                    if l > 0 or not is0(i) or s >= 2:
                        pe.wait_ge(ea_Tc, n - 1)
                    pe.transpose(t_ps[:, s % 2, 0:P], stage[:, s, 0:NEG], ident[:, :]).then_inc(ea_T, 1)
                turn(0, 0)

                def step(i, s, near_end):
                    g = SLOTS * i + s if isinstance(i, int) else None
                    if g is None or g + 1 < NG:
                        turn(i + (s + 1) // SLOTS, (s + 1) % SLOTS)
                    pe.wait_ge(ea_Tc, NG * l + s + 1 + SLOTS * i)
                    if not is0(i) or l:
                        if is0(i):
                            pe.wait_ge(state_done, 3 * COLS * l)
                        else:
                            pe.wait_ge(state_done, 3 * GC * (NG * l + s + 1) + 3 * GC * SLOTS * (i - 1))
                    pe.matmul(h_ps[:, s, :], eaT[:, s % 2, :], bd[:, l, :], start=True, stop=False)
                    pe.wait_ge(got[s], 16 * GC * (uses(l, s, NG) + 1) + 16 * GC * i)
                    pe.matmul(h_ps[:, s, :], ident[:, :], gath[:, s, :], start=False, stop=True).then_inc(h_ready, 1)
                over_groups(pe, step)

                tail = states[:, (NG - 1) % SLOTS, GC - 1, :]
                pe.wait_ge(state_done, 3 * COLS * (l + 1))
                pe.wait_ge(ea_Tc, NG * (l + 1))
                pe.transpose(t_ps[:, 0, 0:P], tail[:, 0:P], ident[:, :]).then_inc(tail_T, 1)
                pe.transpose(t_ps[0:F, 0, P:2 * P], tail[:, P:SW], ident[:, :]).then_inc(tail_T, 1)
                pe.wait_ge(carry_T, l + 1)
                pe.transpose(t_ps[:, 1, 0:P], carryT[:, 0, :], ident[:, :]).then_inc(carry_back, 1)
                pe.transpose(t_ps[:, 1, P:P + F], carryT[0:F, 1, :], ident[0:F, 0:F]).then_inc(carry_back, 1)

            def nodes(l):
                def step(i, s):
                    n = NT * l + s + SLOTS * i
                    pe.wait_ge(mean_ready, n + 1)
                    pe.wait_ge(nx_staged, n + 1)
                    if not is0(i) or l or s >= 2:
                        pe.wait_ge(node_Tc, n - 1)
                    if is0(i) and s < 2:
                        pe.wait_ge(fix_ready, l + 1)
                    pe.transpose(t_ps[:, s % 2, 0:P], agg[:, s, 0:P], ident[:, :]).then_inc(node_T, 1)
                    pe.transpose(t_ps[:, s % 2, P:2 * P], xp[:, s, :], ident[:, :]).then_inc(node_T, 1)
                    pe.wait_ge(node_Tc, n + 1)
                    if not is0(i) or l or s >= 2:
                        pe.wait_ge(node_done, 2 * n - 2)
                    pe.matmul(o_ps[:, s % 2, 0:P], tsb[:, s % 2, 0:P], rw[:, l, 0:2, :].rearrange("p a b -> p (a b)"), start=True, stop=False)
                    pe.matmul(o_ps[:, s % 2, 0:P], tsb[:, s % 2, P:2 * P], rw[:, l, 2:4, :].rearrange("p a b -> p (a b)"), start=False, stop=False)
                    pe.matmul(o_ps[:, s % 2, 0:F], ones[0:1, :], crow[0:1, l, 2, :], start=False, stop=True).then_inc(node_o, 1)
                over_tiles(pe, step)

            def column_sums(bank, tile, done):
                for t in range(0, NT - 1, 8):
                    pe.matmul(h_ps[:, bank, :], ones[:, :], tile[:, t:t + 8, :].rearrange("p a b -> p (a b)"), start=(t == 0), stop=False)
                pe.matmul(h_ps[:, bank, 0:F], ones[0:NL, :], tile[0:NL, NT - 1, :], start=False, stop=True).then_inc(done, 1)

            for l in range(LAYERS):
                edges(l)
                nodes(l)
                pe.wait_ge(node_done, 2 * NT * (l + 1))
                column_sums(0, o_all, mean_ps)
                pe.wait_ge(sq_ready, l + 2)
                column_sums(1, x_all, var_ps)
                if l + 1 < LAYERS:
                    project(l + 1)


_INS = ["x", "src", "dst", "edge_attr_16", "L0_gnn_We", "L0_gnn_be", "L0_gnn_Wpre", "L0_gnn_bpre", "L0_gnn_Wpost",
        "L0_gnn_bpost", "L0_gnn_Wlin", "L0_gnn_blin", "L0_gnn_gamma", "L0_gnn_beta"]


def kernel(**inputs):
    import numpy as _np
    import concourse.bacc as _bacc
    from concourse import mybir as _mybir
    from concourse.bass_utils import run_bass_kernel_spmd as _run

    nc = _bacc.Bacc("TRN2", target_bir_lowering=False, num_devices=1)
    arrays, args = {}, []
    for name in _INS:
        a = _np.ascontiguousarray(inputs[name])
        arrays[f"in_{name}"] = a
        args.append(nc.dram_tensor(f"in_{name}", a.shape, _mybir.dt.from_np(a.dtype), kind="ExternalInput").ap())
    out = nc.dram_tensor("out_0", (N, F), _mybir.dt.float32, kind="ExternalOutput").ap()
    gnn_program(nc, *args, out)
    r = _run(nc, [arrays], core_ids=[0])
    return r.results[0]["out_0"]
```

```python
import concourse.bass as bass
from concourse import mybir
from contextlib import ExitStack

P = 128
N, F, ED, LAYERS = 6250, 64, 16, 2
E = 206250
GC = 8
COLS = -(-E // P)
NG = -(-COLS // GC)
LASTG = COLS - (NG - 1) * GC
LASTC = E - (P - 1) * COLS
SLOTS = 4
NSLOTS = 8
XSLOTS = 4
NT = -(-N // P)
NL = N - (NT - 1) * P
CHUNK = 625
NCH = E // CHUNK
ZROW = P * COLS
SW = 3 * F
NEG = GC * ED
CW = NEG + 2 * GC
BIG = 1.0e38
EPS = 1e-5


def gnn_program(nc, x, src, dst, ea, We, be, Wpre, bpre, Wpost, bpost, Wlin, blin, gamma, beta, out):
    f32, i32 = mybir.dt.float32, mybir.dt.int32
    ALU = mybir.AluOpType
    ACT = mybir.ActivationFunctionType
    AX = mybir.AxisListType

    y_dram = nc.dram_tensor("y_rows", (N, F), f32, kind="Internal").ap()
    st_dram = nc.dram_tensor("edge_states", (ZROW + 1, SW), f32, kind="Internal").ap()

    ctx = ExitStack()
    with ctx:
        def sb(name, shape, dt=f32):
            return ctx.enter_context(nc.sbuf_tensor(name, shape, dt))

        def sem(name):
            return ctx.enter_context(nc.semaphore(name))

        comb = sb("comb", [P, NG, NEG + GC])
        src_all = sb("src_all", [P, COLS], i32)
        x_all = sb("x_all", [P, NT, F])
        o_all = sb("o_all", [P, NT, F])
        states = sb("states", [P, SLOTS, GC, SW])
        rows = sb("rows", [P, SLOTS * CHUNK])
        stage = sb("stage", [P, SLOTS, CW])
        idx = sb("idx", [P, SLOTS, GC], i32)
        eaT = sb("eaT", [P, 2, P])
        tsb = sb("tsb", [P, 2, 2 * P])
        xp = sb("xp", [P, XSLOTS, 2 * F])
        ident = sb("ident", [P, P])
        ones = sb("ones", [P, P])
        shiftm = sb("shiftm", [P, P])
        wrapm = sb("wrapm", [P, P])
        bdmask = sb("bdmask", [P, GC])
        bd = sb("bd", [P, LAYERS, GC * F])
        bd1 = sb("bd1", [P, LAYERS, 2 * F])
        rw = sb("rw", [P, LAYERS, 4, F])
        w64 = sb("w64", [F, LAYERS, 2, F])
        we = sb("we", [ED, LAYERS, F])
        weT = sb("weT", [F, GC, ED])
        bcol = sb("bcol", [F, LAYERS, 2])
        brow = sb("brow", [1, LAYERS, 4, F])
        wide_rows = sb("wide_rows", [P, LAYERS, 5, F])
        nid = sb("nid", [P, NT])
        minus1 = sb("minus1", [P, 1])
        nidh = sb("nidh", [P, NT])
        nidi = sb("nidi", [P, NT], i32)
        le = sb("le", [P, NT])
        chrow = sb("chrow", [P, NT])
        sg = sb("sg", [P, NT])
        ends = sb("ends", [P, NT])
        deg = sb("deg", [P, NT])
        cnt = sb("cnt", [P, NT])
        has = sb("has", [P, NT])
        endf = sb("endf", [P, NT])
        end_i = sb("end_i", [P, NT], i32)
        rcnt = sb("rcnt", [P, NT])
        amp = sb("amp", [P, NT])
        dhi = sb("dhi", [P, 2, NT])
        dint = sb("dint", [P, 3, NT], i32)
        oh = sb("oh", [P, 2, P + NT], mybir.dt.bfloat16)
        small = sb("small", [P, 16])
        fix_i = sb("fix_i", [P, 1], i32)
        pidx_i = sb("pidx_i", [P, 1], i32)
        fixr = sb("fixr", [P, SW])
        links = sb("links", [P, 2, P])
        linkb = sb("linkb", [P, 2, P])
        before = sb("before", [P, 2, P])
        carryT = sb("carryT", [P, 2, P])
        s1 = sb("s1", [P, 4, NT])
        stat = sb("stat", [P, 4, F])
        t1 = sb("t1", [P, 2, F])

        flat = states[:, :, :, :].rearrange("p a b c -> p (a b c)")
        dst_i = flat[:, 0:COLS].bitcast(i32)
        dst_f = flat[:, COLS:2 * COLS]
        same = flat[:, 2 * COLS:3 * COLS]
        fst = flat[0:1, 3 * COLS:3 * COLS + NCH].bitcast(i32)
        fstf = flat[0:1, 3 * COLS + NCH:3 * COLS + 2 * NCH]
        first_b = flat[:, 3 * COLS + 2 * NCH:3 * COLS + 3 * NCH]
        early = stage[:, :, :].rearrange("p a b -> p (a b)")
        wn = early[:, 0:LAYERS * 4 * F].rearrange("p (l a b) -> p l a b", l=LAYERS, a=4)
        iorow = carryT[:, 0, 0:P // 2].bitcast(mybir.dt.bfloat16)
        iorow_i = carryT[:, 1, :].bitcast(i32)
        wT = tsb[0:F, :, :].rearrange("p a b -> p (a b)").rearrange("p (a b) -> p a b", a=4)
        diag2 = tsb[:, 0, :].rearrange("p (a b) -> p a b", a=2)
        zrow = fixr[0:1, :]
        gath = rows[:, 0:SLOTS * GC * F].rearrange("p (s c) -> p s c", s=SLOTS)
        chunks = rows[:, :].bitcast(i32).rearrange("p (s c) -> p s c", s=SLOTS)
        agg = rows[:, 0:NSLOTS * SW].rearrange("p (s c) -> p s c", s=NSLOTS)
        nidx = idx[:, :, :].rearrange("p a b -> p (a b)")
        bcolw = before[0:F, :, :]

        h_ps = ctx.enter_context(nc.psum_tensor("h_ps", [P, 4, 512], f32))
        t_ps = ctx.enter_context(nc.psum_tensor("t_ps", [P, 2, 512], f32))
        o_ps = ctx.enter_context(nc.psum_tensor("o_ps", [P, 2, 512], f32))

        dst_in, src_in, x_loaded, w_in, fst_in = (sem(n) for n in (
            "dst_in", "src_in", "x_loaded", "w_in", "fst_in"))
        ea_in = [sem(f"ea_in{k}") for k in range(3)]
        zero_in, wpost_in = sem("zero_in"), sem("wpost_in")
        act_step, dve_step, pool_step = sem("act_step"), sem("dve_step"), sem("pool_step")
        first_bc, first_ready = sem("first_bc"), sem("first_ready")
        cidx_ready, chunk_counted, le_done = sem("cidx_ready"), sem("chunk_counted"), sem("le_done")
        chunk_got = [sem(f"chunk_got{s}") for s in range(SLOTS)]
        masks_ready = sem("masks_ready")
        w_col, w_t, w_tc, w_p, w_pc = sem("w_col"), sem("w_t"), sem("w_tc"), sem("w_p"), sem("w_pc")
        ends_ready, starts_ps = sem("ends_ready"), sem("starts_ps")
        onehot_ready, onehot_used = sem("onehot_ready"), sem("onehot_used")
        link_in, link_ps, logs_ready, logsum_ps = sem("link_in"), sem("link_ps"), sem("logs_ready"), sem("logsum_ps")
        x_ready, x_chunk, x_relu, x_scaled, pair_staged, pair_T, pair_Tc, pair_y, pair_yc = (sem(n) for n in (
            "x_ready", "x_chunk", "x_relu", "x_scaled", "pair_staged", "pair_T", "pair_Tc", "pair_y", "pair_yc"))
        y_stored = sem("y_stored")
        idx_staged, const_staged, ea_T, ea_Tc, h_ready, state_done = (sem(n) for n in (
            "idx_staged", "const_staged", "ea_T", "ea_Tc", "h_ready", "state_done"))
        got = [sem(f"got{s}") for s in range(SLOTS)]
        stored = [sem(f"stored{s}") for s in range(SLOTS)]
        tail_T, tail_used, carry_T, carry_back = sem("tail_T"), sem("tail_used"), sem("carry_T"), sem("carry_back")
        fix_got, fix_ready, fix_stored = sem("fix_got"), sem("fix_ready"), sem("fix_stored")
        nidx_staged, nx_staged, mean_ready, node_T, node_Tc, node_o, node_done = (sem(n) for n in (
            "nidx_staged", "nx_staged", "mean_ready", "node_T", "node_Tc", "node_o", "node_done"))
        agg_got = [sem(f"agg_got{s}") for s in range(NSLOTS)]
        mean_ps, sq_in, sq_ready, var_ps, var_in, std_ready = (sem(n) for n in (
            "mean_ps", "sq_in", "sq_ready", "var_ps", "var_in", "std_ready"))
        turn = sem("turn")
        res_ready, res_stored = sem("res_ready"), sem("res_stored")

        def linker(eng, s):
            n = [0]

            def link(ins):
                n[0] += 1
                ins.then_inc(s, 1)
                eng.wait_ge(s, n[0])
            return link

        def around(eng, total, slots, step, head=1, tail=1, between={}):
            full = total // slots
            for n in range(head * slots):
                step(n // slots, n % slots)
            cuts = [head, *sorted(between), full - tail]
            for i0, i1 in zip(cuts, cuts[1:]):
                if i0 in between:
                    between[i0]()
                with eng.Fori(i0, i1) as i:
                    for s in range(slots):
                        step(i, s)
            for n in range((full - tail) * slots, total):
                step(n // slots, n % slots)

        def known(i):
            return isinstance(i, int)

        def is0(i):
            return known(i) and i == 0

        def ahead(i, s, k, slots, total):
            if known(i) and slots * i + s + k >= total:
                return None
            return i + (s + k) // slots, (s + k) % slots

        def uses(layer, s, total, slots=SLOTS):
            return layer * len(range(s, total, slots))

        def ea_loads(piece):
            g0, g1 = ea_pieces[piece]
            return 16 * sum((min(g1, c // GC) > g0) + (min(g1, c // GC) < g1 and c % GC > 0) for c in (COLS, COLS, LASTC))

        def columns(i, s):
            return LASTG if known(i) and SLOTS * i + s == NG - 1 else GC

        def rows_got(l, s, i):
            short = GC - LASTG if s == (NG - 1) % SLOTS else 0
            return 16 * (GC * uses(l, s, NG) - short * l + (columns(i, s) - GC) + GC) + 16 * GC * i

        def states_after(l, i, s):
            return 3 * (COLS * l + GC * s + columns(i, s)) + 3 * GC * SLOTS * i

        PAIRS = NT // 2
        STEPS = PAIRS + 1
        ea_pieces = [(0, 64), (64, 128), (128, NG)]
        norm_chunks = [(t, min(t + 8, NT)) for t in range(0, NT, 8)]
        CH = 4
        assert NT == 2 * PAIRS + 1 and NT % NSLOTS == 1 and NCH * CHUNK == E

        def stage_pairs(eng, copy, l, before_put):
            def put(i, s):
                before_put(i, s)
                if known(i) and 2 * i + s == PAIRS:
                    copy(xp[:, s, 0:F], x_all[:, NT - 1, :]).then_inc(pair_staged, 1)
                else:
                    copy(xp[:, s, :], x_all[:, bass.ds(4 * i + 2 * s, 2), :].rearrange("p a b -> p (a b)")).then_inc(pair_staged, 1)

            def take(i, s):
                n = STEPS * l + s
                k = F if known(i) and 2 * i + s == PAIRS else P
                eng.wait_ge(pair_T, n + 1 + 2 * i)
                if l > 0 or not is0(i):
                    eng.wait_ge(pair_y, n - 1 + 2 * i)
                copy(tsb[0:k, s, 0:P], t_ps[0:k, s, 0:P]).then_inc(pair_Tc, 1)

            def first():
                put(0, 0)
                put(0, 1)
                take(0, 0)

            def step(i, s):
                if ahead(i, s, 2, 2, STEPS):
                    put(*ahead(i, s, 2, 2, STEPS))
                if ahead(i, s, 1, 2, STEPS):
                    take(*ahead(i, s, 1, 2, STEPS))
            return first, step

        block = ctx.enter_context(nc.Block())

        @block.sync
        def _(sp):
            sp.dma_start(fst[0:1, :], dst.rearrange("(c k) -> k c", k=CHUNK)[0:1, :], allow_slow_non_contiguous=True).then_inc(fst_in, 16)
            sp.wait_ge(pool_step, 4)
            cut = (P - 1) // 16 * 16

            def load_columns(tile, dram, s):
                v = dram[0:(P - 1) * COLS].rearrange("(p c) -> p c", c=COLS)
                sp.dma_start(tile[0:cut, :], v[0:cut, :]).then_inc(s, 16)
                sp.dma_start(tile[cut:P - 1, :], v[cut:P - 1, :]).then_inc(s, 16)
                sp.dma_start(tile[P - 1:P, 0:LASTC], dram[(P - 1) * COLS:E].rearrange("(p c) -> p c", p=1)).then_inc(s, 16)

            body = ea[0:(P - 1) * COLS, :].rearrange("(p c) k -> p (c k)", c=COLS)
            last = ea[(P - 1) * COLS:E, :].rearrange("(p c) k -> p (c k)", p=1)

            def load_ea(piece):
                g0, g1 = ea_pieces[piece]
                for p0, p1, v, cols in ((0, cut, body, COLS), (cut, P - 1, body, COLS), (P - 1, P, last, LASTC)):
                    q0 = 0 if v is body else P - 1
                    gf = min(g1, cols // GC)
                    if gf > g0:
                        sp.dma_start(comb[p0:p1, g0:gf, 0:NEG],
                                     v[p0 - q0:p1 - q0, g0 * NEG:gf * NEG].rearrange("p (g c) -> p g c", c=NEG)).then_inc(ea_in[piece], 16)
                    if gf < g1 and cols % GC:
                        sp.dma_start(comb[p0:p1, gf, 0:cols % GC * ED],
                                     v[p0 - q0:p1 - q0, gf * NEG:cols * ED]).then_inc(ea_in[piece], 16)

            sp.dma_start(o_all[:, 0:NT - 1, :], x[0:(NT - 1) * P, :].rearrange("(t p) f -> p t f", p=P)).then_inc(x_loaded, 16)
            sp.dma_start(o_all[0:NL, NT - 1, :], x[(NT - 1) * P:N, :]).then_inc(x_loaded, 16)
            for l in range(LAYERS):
                sp.dma_start(w64[:, l, 0, :], Wpre[l, F:2 * F, :]).then_inc(w_in, 16)
                sp.dma_start(w64[:, l, 1, :], Wlin[l, :, :]).then_inc(w_in, 16)
                sp.dma_start(we[:, l, :], We[l, :, :]).then_inc(w_in, 16)
                sp.dma_start(bd1[0:F, l, 0:F], Wpre[l, 0:F, :]).then_inc(w_in, 16)
                sp.dma_start(bd1[F:2 * F, l, F:2 * F], Wpre[l, 0:F, :]).then_inc(w_in, 16)
                sp.dma_start(bcol[:, l, 0:1], be[l, :].rearrange("(f o) -> f o", o=1), allow_slow_non_contiguous=True).then_inc(w_in, 16)
                sp.dma_start(bcol[:, l, 1:2], bpost[l, :].rearrange("(f o) -> f o", o=1), allow_slow_non_contiguous=True).then_inc(w_in, 16)
                for k, b in enumerate((bpre, blin, gamma, beta)):
                    sp.dma_start(brow[0:1, l, k, :], b[l:l + 1, :]).then_inc(w_in, 16)
            sp.wait_ge(dve_step, 1)
            for l in range(LAYERS):
                for half, slot, part in ((0, 0, 3), (1, 0, 2), (0, 1, 6), (1, 1, 5), (0, 2, 1), (1, 2, 0), (0, 3, 4)):
                    sp.dma_start(wn[half * F:(half + 1) * F, l, slot, :],
                                 Wpost[l, part * F:(part + 1) * F, :]).then_inc(wpost_in, 16)
            load_columns(dst_i, dst, dst_in)
            load_columns(src_all, src, src_in)
            sp.dma_start(st_dram[ZROW:ZROW + 1, :], zrow[0:1, :]).then_inc(zero_in, 16)
            sp.wait_ge(chunk_counted, NT)
            load_ea(0)

            st_v = st_dram[0:ZROW, :].rearrange("(p c) w -> p c w", c=COLS)
            for l in range(LAYERS):
                third = (NT - 1) // 3
                for t0 in range(0, NT - 1, third):
                    sp.wait_ge(pair_yc, STEPS * l + (t0 + third) // 2)
                    sp.dma_start(y_dram[t0 * P:(t0 + third) * P, :].rearrange("(t p) f -> p t f", p=P),
                                 o_all[:, t0:t0 + third, :]).then_inc(y_stored, 16)
                sp.wait_ge(pair_yc, STEPS * (l + 1))
                sp.dma_start(y_dram[(NT - 1) * P:N, :], o_all[0:NL, NT - 1, :]).then_inc(y_stored, 16)

                def store(i, s):
                    sp.wait_ge(state_done, states_after(l, i, s))
                    c0, k = GC * SLOTS * i + GC * s, columns(i, s)
                    sp.dma_start(st_v[:, bass.ds(c0, k), :], states[:, s, 0:k, :]).then_inc(stored[s], 16)
                if l == 0:
                    sp.wait_ge(pool_step, 18)
                around(sp, NG, SLOTS, store, tail=0,
                       between={} if l else {2: lambda: load_ea(1), 9: lambda: load_ea(2)})
            sp.wait_ge(var_ps, LAYERS)
            sp.dma_start(x_all[:, 0:NT - 1, :], x[0:(NT - 1) * P, :].rearrange("(t p) f -> p t f", p=P)).then_inc(x_loaded, 16)
            sp.dma_start(x_all[0:NL, NT - 1, :], x[(NT - 1) * P:N, :]).then_inc(x_loaded, 16)
            for k, (t0, t1_) in enumerate(norm_chunks):
                sp.wait_ge(res_ready, k + 1)
                if t1_ < NT:
                    sp.dma_start(out[t0 * P:t1_ * P, :].rearrange("(t p) f -> p t f", p=P), o_all[:, t0:t1_, :]).then_inc(res_stored, 16)
                else:
                    sp.dma_start(out[t0 * P:N, :], o_all[0:NL, t0, :]).then_inc(res_stored, 16)
            sp.wait_ge(res_stored, 16 * len(norm_chunks))
            sp.wait_ge(zero_in, 16)
            for s in range(SLOTS):
                sp.wait_ge(stored[s], 16 * uses(LAYERS, s, NG))
            sp.wait_ge(fix_stored, 16 * LAYERS)

        @block.gpsimd
        def _(pool):
            lg = LASTC // GC
            link = linker(pool, pool_step)
            link(pool.memset(dst_i[96:P, LASTC:COLS], 8191))
            link(pool.memset(src_all[96:P, LASTC:COLS], 0))
            link(pool.memset(o_all[96:P, NT - 1, :], 0.0))
            link(pool.memset(bd1[:, :, :], 0.0))
            link(pool.iota(nidi[:, :], pattern=[[P, NT]], base=0, channel_multiplier=1))
            link(pool.iota(iorow_i[:, :], pattern=[[1, P]], base=0, channel_multiplier=0))
            link(pool.iota(pidx_i[:, :], pattern=[[0, 1]], base=0, channel_multiplier=1))
            link(pool.memset(ident[:, :], 0.0))
            link(pool.memset(shiftm[:, :], 0.0))
            link(pool.memset(wrapm[:, :], 0.0))
            link(pool.memset(bdmask[:, :], 1.0))
            link(pool.affine_select(out=ident[:, :], in_=ident[:, :], compare_op=ALU.not_equal, fill=1.0,
                               base=0, pattern=[[-1, P]], channel_multiplier=1))
            link(pool.affine_select(out=shiftm[:, :], in_=shiftm[:, :], compare_op=ALU.not_equal, fill=1.0,
                               base=-1, pattern=[[1, P]], channel_multiplier=-1))
            link(pool.affine_select(out=wrapm[:, :], in_=wrapm[:, :], compare_op=ALU.not_equal, fill=1.0,
                               base=1 - P, pattern=[[-1, P]], channel_multiplier=1))
            link(pool.affine_select(out=bdmask[:, :], in_=bdmask[:, :], compare_op=ALU.is_ge, fill=0.0,
                               base=0, pattern=[[-ED, GC]], channel_multiplier=1))
            link(pool.affine_select(out=bdmask[:, :], in_=bdmask[:, :], compare_op=ALU.is_ge, fill=0.0,
                               base=ED - 1, pattern=[[ED, GC]], channel_multiplier=-1))

            link(pool.memset(comb[:, NG - 1, :], 0.0))

            dst_ch = dst.rearrange("(c k) -> c k", k=CHUNK)

            def chunk(i, s):
                pool.wait_ge(cidx_ready, SLOTS * i + s + 1)
                if not is0(i):
                    pool.wait_ge(chunk_counted, SLOTS * (i - 1) + s + 1)
                pool.sem_inc(turn, 1)
                pool.indirect_dma_start(chunks[:, s, :], None, dst_ch,
                                        bass.IndirectOffsetOnAxis(ap=idx[:, s, 0:1], axis=0)).then_inc(chunk_got[s], 16)
            around(pool, NT, SLOTS, chunk, tail=0)
            link(pool.memset(comb[96:P, LASTC // GC:NG - 1, 0:NEG], 0.0))

            for l in range(LAYERS):
                pool.wait_ge(y_stored, 64 * (l + 1))
                if l == 0:
                    pool.wait_ge(chunk_counted, NT)
                else:
                    pool.wait_ge(node_T, 2 * NT * l)
                    pool.wait_ge(mean_ready, NT * l)

                def gather(i, s):
                    pool.wait_ge(idx_staged, NG * l + s + 1 + SLOTS * i)
                    if not is0(i):
                        pool.wait_ge(h_ready, NG * l + s + 1 + SLOTS * (i - 1))
                    pool.sem_inc(turn, 1)
                    for c in range(columns(i, s)):
                        pool.indirect_dma_start(gath[:, s, c * F:(c + 1) * F], None, y_dram,
                                                bass.IndirectOffsetOnAxis(ap=idx[:, s, c:c + 1], axis=0)).then_inc(got[s], 16)
                around(pool, NG, SLOTS, gather, tail=0)

                for s in range(SLOTS):
                    pool.wait_ge(stored[s], 16 * uses(l + 1, s, NG))
                pool.wait_ge(zero_in, 16)
                pool.indirect_dma_start(fixr[:, :], None, st_dram,
                                        bass.IndirectOffsetOnAxis(ap=fix_i[:, 0:1], axis=0)).then_inc(fix_got, 16)
                pool.wait_ge(fix_ready, l + 1)
                pool.indirect_dma_start(st_dram, bass.IndirectOffsetOnAxis(ap=fix_i[:, 0:1], axis=0),
                                        fixr[:, :], None).then_inc(fix_stored, 16)
                pool.wait_ge(fix_stored, 16 * (l + 1))
                pool.wait_ge(h_ready, NG * (l + 1))

                def node_rows(i, s):
                    n = NT * l + s
                    pool.wait_ge(nidx_staged, n + 1 + NSLOTS * i)
                    if not is0(i):
                        pool.wait_ge(node_T, 2 * (n + 1) + 2 * NSLOTS * (i - 1))
                        pool.wait_ge(mean_ready, n + 1 + NSLOTS * (i - 1))
                    pool.sem_inc(turn, 1)
                    pool.indirect_dma_start(agg[:, s, :], None, st_dram,
                                            bass.IndirectOffsetOnAxis(ap=nidx[:, s:s + 1], axis=0)).then_inc(agg_got[s], 16)
                around(pool, NT, NSLOTS, node_rows, tail=0)

        @block.scalar
        def _(act):
            link = linker(act, act_step)

            def stage_chunk(i, s):
                act.wait_ge(le_done, SLOTS * i + s + 1)
                act.activation(idx[:, s, 0:1], le[:, bass.ds(SLOTS * i + s, 1)], ACT.Relu, bias=minus1[:, 0:1]).then_inc(cidx_ready, 1)

            def count(i, s):
                act.wait_ge(chunk_got[s], 16 * i + 16)
                t = SLOTS * i + s
                act.activation(chunks[:, s, :].bitcast(f32), chunks[:, s, :], ACT.Sign, bias=nidh[:, bass.ds(t, 1)],
                               scale=-1.0, accum_out=sg[:, bass.ds(t, 1)]).then_inc(chunk_counted, 1)

            def chunk_step(i, s):
                count(i, s)
                if ahead(i, s, SLOTS, SLOTS, NT):
                    stage_chunk(i + 1, s)

            full, half = NT // SLOTS, NT // SLOTS // 2
            for s in range(SLOTS):
                stage_chunk(0, s)
            for s in range(SLOTS):
                chunk_step(0, s)
            with act.Fori(1, half) as i:
                for s in range(SLOTS):
                    chunk_step(i, s)
            act.wait_ge(sq_in, 1)
            act.activation(o_all[:, :, :], x_all[:, :, :], ACT.Square).then_inc(sq_ready, 1)
            act.wait_ge(var_in, 1)
            act.activation(s1[:, 2, :], s1[:, 1, :], ACT.Sqrt).then_inc(std_ready, 1)
            with act.Fori(half, full - 1) as i:
                for s in range(SLOTS):
                    chunk_step(i, s)
            for n in range((full - 1) * SLOTS, NT):
                chunk_step(n // SLOTS, n % SLOTS)

            def edges(l):
                def stage_idx(i, s):
                    k = columns(i, s)
                    act.copy(idx[:, s, 0:k], src_all[:, bass.ds(GC * SLOTS * i + GC * s, k)]).then_inc(idx_staged, 1)

                def stage_const(i, s):
                    g = bass.ds(SLOTS * i + s, 1)
                    act.copy(stage[:, s, 0:NEG + GC], comb[:, g, :].rearrange("p o c -> p (o c)"))
                    act.activation(stage[:, s, NEG + GC:CW], comb[:, g, NEG:NEG + GC].rearrange("p o c -> p (o c)"),
                                   ACT.Copy, bias=-BIG, scale=BIG).then_inc(const_staged, 1)

                def take(i, s):
                    n = NG * l + s + SLOTS * i
                    act.wait_ge(ea_T, n + 1)
                    if l > 0 or not is0(i) or s >= 2:
                        act.wait_ge(h_ready, n - 1)
                    act.copy(eaT[:, s % 2, :], t_ps[:, s % 2, 0:P]).then_inc(ea_Tc, 1)
                for s in range(SLOTS):
                    stage_idx(0, s)
                    stage_const(0, s)
                take(0, 0)

                def step(i, s):
                    if ahead(i, s, 1, SLOTS, NG):
                        take(*ahead(i, s, 1, SLOTS, NG))
                    if ahead(i, s, SLOTS, SLOTS, NG):
                        act.wait_ge(got[s], rows_got(l, s, i))
                        stage_idx(i + 1, s)
                        act.wait_ge(state_done, states_after(l, i, s))
                        stage_const(i + 1, s)
                around(act, NG, SLOTS, step, between={} if l else {
                    g0 // SLOTS - 1: (lambda k: lambda: act.wait_ge(ea_in[k], ea_loads(k)))(k)
                    for k, (g0, _) in enumerate(ea_pieces) if k})

            def nodes(l):
                def stage_idx(i, s):
                    act.copy(nidx[:, s:s + 1], end_i[:, bass.ds(NSLOTS * i + s, 1)]).then_inc(nidx_staged, 1)

                def stage_x(i, s):
                    act.copy(xp[:, s % XSLOTS, F:2 * F], x_all[:, bass.ds(NSLOTS * i + s, 1), :].rearrange("p o c -> p (o c)")).then_inc(nx_staged, 1)

                for s in range(SLOTS):
                    act.wait_ge(got[s], rows_got(l, s, (NG - 1 - s) // SLOTS))
                for s in range(NSLOTS):
                    stage_idx(0, s)
                for s in range(XSLOTS):
                    stage_x(0, s)

                def step(i, s):
                    n = NT * l + s
                    act.wait_ge(node_T, 2 * n + 2 + 2 * NSLOTS * i)
                    if l > 0 or not is0(i) or s >= 2:
                        act.wait_ge(node_o, n - 1 + NSLOTS * i)
                    act.copy(tsb[:, s % 2, :], t_ps[:, s % 2, 0:2 * P]).then_inc(node_Tc, 1)
                    if ahead(i, s, XSLOTS, NSLOTS, NT):
                        stage_x(*ahead(i, s, XSLOTS, NSLOTS, NT))
                    if ahead(i, s, NSLOTS, NSLOTS, NT):
                        stage_idx(i + 1, s)
                around(act, NT, NSLOTS, step)

            def logs():
                act.wait_ge(onehot_used, NT)
                act.activation(small[:, 8:9], o_ps[:, 0, NT - 1:NT], ACT.Ln, bias=1.0).then_inc(act_step, 1)
                act.activation(dhi[:, 0, 0:NT - 1], o_ps[:, 0, 0:NT - 1], ACT.Ln, bias=1.0, accum_out=small[:, 9:10]).then_inc(logs_ready, 1)
                act.activation(amp[:, :], cnt[:, :], ACT.Ln, bias=1.0).then_inc(logs_ready, 1)

            def norm(l):
                for k, (t0, t1_) in enumerate(norm_chunks):
                    act.wait_ge(sq_in, 1 + len(norm_chunks) * l + k + 1)
                    act.activation(x_all[:, t0:t1_, :], o_all[:, t0:t1_, :], ACT.Square).then_inc(sq_ready, 1)
                act.wait_ge(var_in, l + 2)
                act.activation(stat[:, 2, :], stat[:, 1, :], ACT.Sqrt).then_inc(std_ready, 1)

            def project(l):
                def relu(i, s):
                    if s:
                        return
                    act.wait_ge(x_chunk, i + 1)
                    k = 1 if known(i) and CH * i == NT - 1 else CH
                    act.activation(x_all[:, bass.ds(CH * i, k), :], o_all[:, bass.ds(CH * i, k), :], ACT.Relu).then_inc(x_relu, 1)
                    act.wait_ge(x_relu, i + 1)
                    act.sem_inc(turn, 1)
                first, step = stage_pairs(act, act.copy, l, relu)
                first()
                around(act, STEPS, 2, step)

            act.wait_ge(masks_ready, 1 + (LASTG < GC))
            act.wait_ge(src_in, 48)
            act.wait_ge(ea_in[0], ea_loads(0))
            for l in range(LAYERS):
                edges(l)
                if l == 0:
                    logs()
                nodes(l)
                norm(l)
                if l + 1 < LAYERS:
                    project(l + 1)

        @block.vector
        def _(dve):
            link = linker(dve, dve_step)

            def wide(ap):
                return ap.unsqueeze(2).broadcast_to([P, NT, F])

            dve.memset(ones[:, :], 1.0).then_inc(first_bc, 1)
            dve.memset(minus1[:, :], -1.0)
            dve.memset(zrow[:, :], 0.0)
            link(dve.memset(wn[:, :, 3, :], 0.0))
            dve.wait_ge(fst_in, 16)
            dve.tensor_copy(fstf[0:1, :], fst[0:1, :]).then_inc(first_bc, 1)
            dve.wait_ge(pool_step, 16)
            link(dve.tensor_copy(nid[:, :], nidi[:, :]))
            dve.tensor_scalar(nidh[:, :], nid[:, :], 0.5, None, ALU.add)
            link(dve.tensor_copy(iorow[:, :], iorow_i[:, :]))
            dve.wait_ge(first_ready, 1)
            link(dve.tensor_copy(first_b[:, :], o_ps[:, 0, 0:NCH]))

            def le_step(i, s):
                t = SLOTS * i + s
                if s >= 2 or not is0(i):
                    dve.wait_ge(le_done, t - 1)
                dve.tensor_scalar(o_ps[:, s % 2, 0:NCH], first_b[:, :], nid[:, bass.ds(t, 1)], None,
                                  ALU.is_le, ALU.add, accum_out=le[:, bass.ds(t, 1)]).then_inc(le_done, 1)
            around(dve, NT, SLOTS, le_step, tail=0)
            dve.wait_ge(x_loaded, 32)
            link(dve.tensor_reduce(s1[:, 0, :], o_all[:, :, :], AX.X, ALU.add))
            link(dve.tensor_scalar(s1[:, 0, :], s1[:, 0, :], 1.0 / F, None, ALU.mult))
            dve.tensor_tensor(x_all[:, :, :], o_all[:, :, :], wide(s1[:, 0, :]), ALU.subtract).then_inc(sq_in, 1)
            for l in range(LAYERS):
                dve.wait_ge(w_in, 16 * 11 * LAYERS)
                if l:
                    dve.wait_ge(w_p, 4 * l)
                dve.tensor_copy(bcolw[:, :, :], bcol[:, l, :].unsqueeze(2).broadcast_to([F, 2, P])).then_inc(w_col, 1)
                dve.wait_ge(w_t, 2 * l + 1)
                dve.tensor_copy(weT[:, :, :], h_ps[0:F, 0, 0:ED].unsqueeze(1).broadcast_to([F, GC, ED])).then_inc(w_tc, 1)
                dve.wait_ge(w_t, 2 * l + 2)
                dve.tensor_copy(wT[:, :, :], h_ps[0:F, 1, :].rearrange("p (a b) -> p a b", a=4)).then_inc(w_tc, 1)
                dve.wait_ge(w_p, 4 * l + 4)
                dve.tensor_tensor(bd[:, l, :].rearrange("p (j f) -> p j f", j=GC),
                                  h_ps[:, 2, 0:F].unsqueeze(1).broadcast_to([P, GC, F]),
                                  bdmask[:, :].unsqueeze(2).broadcast_to([P, GC, F]), ALU.mult)
                dve.tensor_copy(rw[:, l, :, :], h_ps[:, 3, 0:4 * F].rearrange("p (a b) -> p a b", a=4))
                dve.tensor_copy(wide_rows[:, l, 0:3, :], h_ps[:, 2, F:4 * F].rearrange("p (a b) -> p a b", a=3))
                dve.tensor_copy(wide_rows[:, l, 3:5, :], h_ps[:, 3, 4 * F:6 * F].rearrange("p (a b) -> p a b", a=2)).then_inc(w_pc, 1)

            dve.wait_ge(sq_ready, 1)
            link(dve.tensor_reduce(s1[:, 1, :], o_all[:, :, :], AX.X, ALU.add))
            dve.tensor_scalar(s1[:, 1, :], s1[:, 1, :], 1.0 / F, EPS, ALU.mult, ALU.add).then_inc(var_in, 1)
            dve.wait_ge(std_ready, 1)
            link(dve.reciprocal(s1[:, 3, :], s1[:, 2, :]))
            link(dve.tensor_tensor(x_all[:, :, :], x_all[:, :, :], wide(s1[:, 3, :]), ALU.mult))
            dve.tensor_scalar(x_all[:, :, :], x_all[:, :, :], 0.0, None, ALU.max).then_inc(x_ready, 1)

            def y_out(l, i, s):
                dve.wait_ge(pair_y, STEPS * l + s + 1 + 2 * i)
                k = 1 if known(i) and 2 * i + s == PAIRS else 2
                dve.tensor_tensor(o_all[:, bass.ds(4 * i + 2 * s, k), :].rearrange("p a b -> p (a b)"), o_ps[:, s, 0:k * F],
                                  wide_rows[:, l, 0:k, :].rearrange("p a b -> p (a b)"), ALU.add).then_inc(pair_yc, 1)

            dve.wait_ge(x_ready, 1)
            dve.wait_ge(w_pc, LAYERS)
            first, pair_step = stage_pairs(dve, dve.tensor_copy, 0, lambda i, s: None)
            first()

            def first_y(i, s):
                pair_step(i, s)
                y_out(0, i, s)
            around(dve, STEPS, 2, first_y)

            dve.wait_ge(dst_in, 48)
            link(dve.tensor_copy(dst_f[:, :], dst_i[:, :]))
            dve.memset(same[:, 0:1], 0.0)
            link(dve.tensor_tensor(same[:, 1:COLS], dst_f[:, 1:COLS], dst_f[:, 0:COLS - 1], ALU.is_equal))
            gf = COLS // GC
            dve.tensor_copy(comb[:, 0:gf, NEG:NEG + GC], same[:, 0:gf * GC].rearrange("p (g c) -> p g c", c=GC)).then_inc(masks_ready, 1)
            if gf < NG:
                dve.tensor_copy(comb[:, gf, NEG:NEG + LASTG], same[:, gf * GC:COLS]).then_inc(masks_ready, 1)
            dve.tensor_copy(small[:, 0:1], dst_f[:, 0:1])
            link(dve.tensor_copy(small[:, 1:2], dst_f[:, COLS - 1:COLS]))
            link(dve.tensor_scalar(same, dst_f, small[:, 0:1], None, ALU.is_equal, ALU.add, accum_out=small[:, 2:3]))
            link(dve.tensor_copy(small[:, 3:4], pidx_i[:, 0:1]))
            dve.tensor_scalar(small[:, 4:5], small[:, 3:4], float(COLS), -1.0, ALU.mult, ALU.add)
            link(dve.tensor_scalar(small[:, 12:13], small[:, 3:4], 1.0, None, ALU.min))
            link(dve.tensor_tensor(small[:, 5:6], small[:, 4:5], small[:, 2:3], ALU.add))
            link(dve.tensor_copy(fix_i[:, :], small[:, 5:6]))
            dve.memset(states[:, SLOTS - 1, GC - 1, :], 0.0).then_inc(link_in, 1)
            dve.wait_ge(link_ps, 1)
            link(dve.tensor_copy(small[:, 6:8], o_ps[:, 1, 0:2]))
            dve.tensor_tensor(small[:, 10:11], small[:, 7:8], small[:, 0:1], ALU.is_equal)
            link(dve.tensor_tensor(small[:, 11:12], small[:, 7:8], small[:, 6:7], ALU.is_equal))
            link(dve.tensor_tensor(small[:, 10:11], small[:, 10:11], small[:, 12:13], ALU.mult))
            link(dve.tensor_tensor(small[:, 11:12], small[:, 10:11], small[:, 11:12], ALU.mult))
            dve.tensor_scalar(diag2[:, 0, :], ident[:, :], small[:, 10:11], None, ALU.mult)
            dve.tensor_scalar(diag2[:, 1, :], ident[:, :], small[:, 11:12], None, ALU.mult).then_inc(link_in, 1)
            dve.wait_ge(link_ps, 2)
            link(dve.tensor_copy(links[:, :, :], o_ps[:, 1, 0:2 * P].rearrange("p (a b) -> p a b", a=2)))
            dve.tensor_scalar(linkb[0:F, :, :], links[0:F, :, :], -1.0, BIG, ALU.add, ALU.mult)
            dve.tensor_scalar(linkb[F:P, :, :], links[F:P, :, :], -1.0, -BIG, ALU.add, ALU.mult)
            dve.memset(before[0:F, 0, 0:1], -BIG)
            dve.memset(before[F:P, 0, 0:1], BIG)
            link(dve.memset(before[0:F, 1, 0:1], 0.0))

            dve.wait_ge(chunk_counted, NT)
            link(dve.tensor_scalar(ends[:, :], sg[:, :], float(CHUNK), 0.5, ALU.add, ALU.mult))
            link(dve.tensor_scalar(chrow[:, :], le[:, :], -1.0, 0.0, ALU.add, ALU.max))
            link(dve.tensor_scalar(chrow[:, :], chrow[:, :], float(CHUNK), None, ALU.mult))
            dve.tensor_tensor(ends[:, :], ends[:, :], chrow[:, :], ALU.add).then_inc(ends_ready, 1)
            dve.wait_ge(starts_ps, 1)
            link(dve.tensor_tensor(deg[:, :], ends[:, :], o_ps[:, 1, 0:NT], ALU.subtract))
            dve.tensor_scalar(has[:, :], deg[:, :], 1.0, None, ALU.min)
            dve.tensor_scalar(cnt[:, :], deg[:, :], 1.0, None, ALU.max)
            link(dve.tensor_scalar(endf[:, :], ends[:, :], -1.0 - ZROW, None, ALU.add))
            link(dve.reciprocal(rcnt[:, :], cnt[:, :]))
            link(dve.tensor_tensor(endf[:, :], endf[:, :], has[:, :], ALU.mult))
            link(dve.tensor_scalar(endf[:, :], endf[:, :], float(ZROW), None, ALU.add))
            link(dve.tensor_copy(end_i[:, :], endf[:, :]))
            link(dve.tensor_copy(dint[:, 0, :], deg[:, :]))
            dve.tensor_scalar(dint[:, 1, :], dint[:, 0, :], 7, None, ALU.logical_shift_right)
            link(dve.tensor_scalar(dint[:, 2, :], dint[:, 0, :], P - 1, None, ALU.bitwise_and))
            link(dve.tensor_copy(dhi[:, :, :], dint[:, 1:3, :]))

            def one_hot(i, s):
                t = SLOTS * i + s
                if s >= 2 or not is0(i):
                    dve.wait_ge(onehot_used, t - 1)
                dve.tensor_scalar(oh[:, s % 2, 0:P], iorow[:, :], dhi[:, 1, bass.ds(t, 1)], None, ALU.is_equal)
                dve.tensor_scalar(oh[:, s % 2, P:P + NT], iorow[:, 0:NT], dhi[:, 0, bass.ds(t, 1)], None, ALU.is_equal).then_inc(onehot_ready, 1)
            around(dve, NT, SLOTS, one_hot, tail=0)

            def amplify():
                dve.wait_ge(logs_ready, 2)
                dve.wait_ge(logsum_ps, 1)
                link(dve.tensor_reduce(small[:, 13:14], o_ps[:, 1, 0:2], AX.X, ALU.add))
                link(dve.tensor_scalar(small[:, 14:15], small[:, 13:14], 1.0 / N, None, ALU.mult))
                link(dve.reciprocal(small[:, 15:16], small[:, 14:15]))
                link(dve.tensor_scalar(amp[:, :], amp[:, :], small[:, 15:16], None, ALU.mult))

            def edges(l):
                def step(i, s):
                    dve.wait_ge(h_ready, NG * l + s + 1 + SLOTS * i)
                    if l > 0 or not is0(i):
                        dve.wait_ge(stored[s], 16 * uses(l, s, NG) + 16 * i)
                    for c in range(columns(i, s)):
                        n = 3 * (COLS * l + GC * s + c)
                        if l > 0 or not is0(i) or s or c:
                            dve.wait_ge(state_done, n + 3 * GC * SLOTS * i)
                        last = states[:, s, c - 1, :] if c else states[:, (s - 1) % SLOTS, GC - 1, :]
                        h = h_ps[:, s, c * F:(c + 1) * F]
                        one = stage[:, s, NEG + c:NEG + c + 1]
                        neg = stage[:, s, NEG + GC + c:NEG + GC + c + 1]
                        for k, (mask, op0, op1) in enumerate(((neg, ALU.add, ALU.max), (neg, ALU.subtract, ALU.min),
                                                              (one, ALU.mult, ALU.add))):
                            dve.scalar_tensor_tensor(out=states[:, s, c, k * F:(k + 1) * F], in0=last[:, k * F:(k + 1) * F],
                                                     scalar=mask, in1=h, op0=op0, op1=op1).then_inc(state_done, 1)
                around(dve, NG, SLOTS, step, tail=0)

                dve.wait_ge(tail_T, 2 * l + 2)
                dve.tensor_tensor(before[:, 0, 1:P], t_ps[:, 0, 0:P - 1], linkb[:, 0, 1:P], ALU.add)
                link(dve.tensor_tensor(before[0:F, 1, 1:P], t_ps[0:F, 0, P:2 * P - 1], links[0:F, 0, 1:P], ALU.mult))
                dve.tensor_tensor_scan(carryT[0:F, 0, :], linkb[0:F, 1, :], before[0:F, 0, :], -BIG, ALU.add, ALU.max)
                dve.tensor_tensor_scan(carryT[F:P, 0, :], linkb[F:P, 1, :], before[F:P, 0, :], BIG, ALU.add, ALU.min)
                dve.tensor_tensor_scan(carryT[0:F, 1, :], links[0:F, 1, :], before[0:F, 1, :], 0.0, ALU.mult, ALU.add).then_inc(carry_T, 1)
                dve.wait_ge(carry_back, 2 * l + 2)
                dve.wait_ge(fix_got, 16 * (l + 1))
                dve.tensor_tensor(fixr[:, 0:F], fixr[:, 0:F], t_ps[:, 1, 0:F], ALU.max)
                dve.tensor_tensor(fixr[:, F:2 * F], fixr[:, F:2 * F], t_ps[:, 1, F:2 * F], ALU.min)
                dve.tensor_tensor(fixr[:, 2 * F:SW], fixr[:, 2 * F:SW], t_ps[:, 1, 2 * F:SW], ALU.add).then_inc(fix_ready, 1)

            def nodes(l):
                def mean(i, s):
                    n = NT * l + s
                    dve.wait_ge(agg_got[s], 16 * uses(l, s, NT, NSLOTS) + 16 + 16 * i)
                    if l > 0 or not is0(i) or s >= XSLOTS:
                        dve.wait_ge(node_T, 2 * (n + 1 - XSLOTS) + 2 * NSLOTS * i)
                    dve.tensor_scalar(xp[:, s % XSLOTS, 0:F], agg[:, s, 2 * F:SW], rcnt[:, bass.ds(NSLOTS * i + s, 1)], None, ALU.mult).then_inc(mean_ready, 1)

                def output(i, s):
                    n = NT * l + s
                    t = NSLOTS * i + s
                    dve.wait_ge(node_o, n + 1 + NSLOTS * i)
                    dve.scalar_tensor_tensor(out=t1[:, s % 2, :], in0=o_ps[:, s % 2, F:2 * F], scalar=amp[:, bass.ds(t, 1)],
                                             in1=wide_rows[:, l, 2, :], op0=ALU.mult, op1=ALU.add).then_inc(node_done, 1)
                    dve.wait_ge(node_done, 2 * n + 1 + 2 * NSLOTS * i)
                    dve.tensor_tensor(o_all[:, bass.ds(t, 1), :].rearrange("p o c -> p (o c)"), o_ps[:, s % 2, 0:F], t1[:, s % 2, :], ALU.add).then_inc(node_done, 1)

                def step(i, s):
                    if ahead(i, s, 2, NSLOTS, NT):
                        mean(*ahead(i, s, 2, NSLOTS, NT))
                    output(i, s)
                mean(0, 0)
                mean(0, 1)
                around(dve, NT, NSLOTS, step)

            def norm(l, last):
                dve.wait_ge(mean_ps, l + 1)
                link(dve.tensor_reduce(stat[:, 0, :], h_ps[:, 0, :].rearrange("p (a f) -> p f a", f=F), AX.X, ALU.add))
                link(dve.tensor_scalar(stat[:, 0, :], stat[:, 0, :], 1.0 / N, None, ALU.mult))

                def rows_of(ap, k):
                    return ap.unsqueeze(1).broadcast_to([P, k, F])
                for t0, t1_ in norm_chunks:
                    o = o_all[:, t0:t1_, :]
                    dve.tensor_tensor(o, o, rows_of(stat[:, 0, :], t1_ - t0), ALU.subtract).then_inc(sq_in, 1)
                dve.wait_ge(var_ps, l + 1)
                link(dve.tensor_reduce(stat[:, 1, :], h_ps[:, 1, :].rearrange("p (a f) -> p f a", f=F), AX.X, ALU.add))
                dve.tensor_scalar(stat[:, 1, :], stat[:, 1, :], 1.0 / N, EPS, ALU.mult, ALU.add).then_inc(var_in, 1)
                dve.wait_ge(std_ready, l + 2)
                link(dve.reciprocal(stat[:, 3, :], stat[:, 2, :]))
                link(dve.tensor_tensor(stat[:, 3, :], stat[:, 3, :], wide_rows[:, l, 3, :], ALU.mult))
                if last:
                    dve.wait_ge(x_loaded, 64)
                    for t0, t1_ in norm_chunks:
                        o, k = o_all[:, t0:t1_, :], t1_ - t0
                        link(dve.tensor_tensor(o, o, rows_of(stat[:, 3, :], k), ALU.mult))
                        link(dve.tensor_tensor(o, o, rows_of(wide_rows[:, l, 4, :], k), ALU.add))
                        dve.scalar_tensor_tensor(out=o, in0=o, scalar=0.0, in1=x_all[:, t0:t1_, :],
                                                 op0=ALU.max, op1=ALU.add).then_inc(res_ready, 1)
                    return

                def scale(i):
                    k = 1 if known(i) and CH * i == NT - 1 else CH
                    o = o_all[:, bass.ds(CH * i, k), :]
                    dve.tensor_tensor(o, o, rows_of(stat[:, 3, :], k), ALU.mult).then_inc(x_scaled, 1)
                    dve.wait_ge(x_scaled, i + 1)
                    dve.tensor_tensor(o, o, rows_of(wide_rows[:, l, 4, :], k), ALU.add).then_inc(x_chunk, 1)

                def step(i, s):
                    if s == 0 and not (known(i) and CH * (i + 2) >= NT):
                        scale(i + 2)
                    y_out(l + 1, i, s)
                scale(0)
                scale(1)
                around(dve, STEPS, 2, step, tail=2)

            for l in range(LAYERS):
                edges(l)
                if l == 0:
                    amplify()
                nodes(l)
                norm(l, l + 1 == LAYERS)

        @block.tensor
        def _(pe):
            pe.wait_ge(first_bc, 2)
            pe.matmul(o_ps[:, 0, 0:NCH], ones[0:1, :], fstf[0:1, :], start=True, stop=True).then_inc(first_ready, 1)

            pe.wait_ge(pool_step, 16)
            small_loads, row_loads = 11 * LAYERS, 7
            pe.wait_ge(dve_step, 1)
            for l in range(LAYERS):
                pe.wait_ge(w_in, 16 * small_loads)
                pe.wait_ge(wpost_in, 16 * row_loads * LAYERS)
                if l:
                    pe.wait_ge(w_pc, l)
                pe.transpose(h_ps[0:F, 0, 0:ED], we[:, l, :], ident[0:ED, 0:ED]).then_inc(w_t, 1)
                for k in range(4):
                    t = pe.transpose(h_ps[0:F, 1, k * P:(k + 1) * P], wn[:, l, k, :], ident[:, :])
                t.then_inc(w_t, 1)
                pe.wait_ge(w_tc, 2 * l + 2)
                pe.matmul(h_ps[:, 2, 0:F], weT[:, :, :].rearrange("p a b -> p (a b)"), w64[:, l, 0, :], start=True, stop=True).then_inc(w_p, 1)
                for k in range(4):
                    m = pe.matmul(h_ps[:, 3, k * F:(k + 1) * F], wT[:, k, :], w64[:, l, 1, :], start=True, stop=True)
                m.then_inc(w_p, 1)
                pe.wait_ge(w_col, l + 1)
                for k, j in enumerate((0, 0, 1)):
                    to = h_ps[:, 2, (k + 1) * F:(k + 2) * F]
                    pe.matmul(to, bcolw[:, j, :], w64[:, l, j, :], start=True, stop=False)
                    m = pe.matmul(to, ones[0:1, :], brow[0:1, l, j, :], start=False, stop=True)
                m.then_inc(w_p, 1)
                pe.matmul(h_ps[:, 3, 4 * F:6 * F], ones[0:1, :], brow[0:1, l, 2:4, :].rearrange("p a b -> p (a b)"), start=True, stop=True).then_inc(w_p, 1)

            def project(l):
                def turn(i, s):
                    n = STEPS * l + s
                    pe.wait_ge(pair_staged, n + 1 + 2 * i)
                    if not is0(i) or l:
                        pe.wait_ge(pair_Tc, n - 1 + 2 * i)
                    if known(i) and 2 * i + s == PAIRS:
                        pe.transpose(t_ps[0:F, s, 0:P], xp[:, s, 0:F], ident[:, :]).then_inc(pair_T, 1)
                    else:
                        pe.transpose(t_ps[:, s, 0:P], xp[:, s, :], ident[:, :]).then_inc(pair_T, 1)

                def step(i, s):
                    n = STEPS * l + s
                    if ahead(i, s, 1, 2, STEPS):
                        turn(*ahead(i, s, 1, 2, STEPS))
                    pe.wait_ge(pair_Tc, n + 1 + 2 * i)
                    if not is0(i) or l:
                        pe.wait_ge(pair_yc, n - 1 + 2 * i)
                    k = F if known(i) and 2 * i + s == PAIRS else P
                    pe.matmul(o_ps[:, s, 0:k], tsb[0:k, s, 0:P], bd1[0:k, l, 0:k], start=True, stop=True).then_inc(pair_y, 1)
                turn(0, 0)
                around(pe, STEPS, 2, step)

            pe.wait_ge(w_pc, LAYERS)
            pe.wait_ge(le_done, NT)
            project(0)

            pe.wait_ge(pair_yc, PAIRS + 1)
            pe.wait_ge(link_in, 1)
            pe.matmul(o_ps[:, 1, 0:2], shiftm[:, :], small[:, 0:2], start=True, stop=True).then_inc(link_ps, 1)
            pe.wait_ge(link_in, 2)
            pe.matmul(o_ps[:, 1, 0:2 * P], ones[:, :], diag2[:, :, :].rearrange("p a b -> p (a b)"), start=True, stop=True).then_inc(link_ps, 1)
            pe.wait_ge(ends_ready, 1)
            pe.matmul(o_ps[:, 1, 0:NT], shiftm[:, :], ends[:, :], start=True, stop=False)
            pe.matmul(o_ps[:, 1, 1:NT], wrapm[:, :], ends[:, 0:NT - 1], start=False, stop=True).then_inc(starts_ps, 1)

            def hist(i, s):
                t = SLOTS * i + s
                pe.wait_ge(onehot_ready, t + 1)
                k = NL if isinstance(i, int) and t == NT - 1 else P
                last = isinstance(i, int) and t == NT - 1
                m = pe.matmul(o_ps[:, 0, 0:NT], oh[0:k, s % 2, 0:P], oh[0:k, s % 2, P:P + NT], start=isinstance(i, int) and t == 0, stop=last)
                m.then_inc(onehot_used, 1)
            around(pe, NT, SLOTS, hist, tail=0)

            def log_sum():
                pe.wait_ge(logs_ready, 2)
                pe.wait_ge(act_step, 1)
                pe.matmul(o_ps[:, 1, 0:1], ones[0:NL, :], small[0:NL, 8:9], start=True, stop=True)
                pe.matmul(o_ps[:, 1, 1:2], ones[:, :], small[:, 9:10], start=True, stop=True).then_inc(logsum_ps, 1)

            def edges(l):
                def turn(i, s):
                    n = NG * l + s + SLOTS * i
                    pe.wait_ge(const_staged, n + 1)
                    if l > 0 or not is0(i) or s >= 2:
                        pe.wait_ge(ea_Tc, n - 1)
                    pe.transpose(t_ps[:, s % 2, 0:P], stage[:, s, 0:NEG], ident[:, :]).then_inc(ea_T, 1)
                turn(0, 0)

                def step(i, s):
                    if ahead(i, s, 1, SLOTS, NG):
                        turn(*ahead(i, s, 1, SLOTS, NG))
                    pe.wait_ge(ea_Tc, NG * l + s + 1 + SLOTS * i)
                    if not is0(i) or l:
                        if is0(i):
                            pe.wait_ge(state_done, 3 * COLS * l)
                        else:
                            pe.wait_ge(state_done, 3 * (COLS * l + GC * (s + 1)) + 3 * GC * SLOTS * (i - 1))
                    pe.matmul(h_ps[:, s, :], eaT[:, s % 2, :], bd[:, l, :], start=True, stop=False)
                    pe.wait_ge(got[s], rows_got(l, s, i))
                    pe.matmul(h_ps[:, s, :], ident[:, :], gath[:, s, :], start=False, stop=True).then_inc(h_ready, 1)
                around(pe, NG, SLOTS, step)

                tail = states[:, (NG - 1) % SLOTS, LASTG - 1, :]
                pe.wait_ge(state_done, 3 * COLS * (l + 1))
                pe.wait_ge(ea_Tc, NG * (l + 1))
                pe.transpose(t_ps[:, 0, 0:P], tail[:, 0:P], ident[:, :]).then_inc(tail_T, 1)
                pe.transpose(t_ps[0:F, 0, P:2 * P], tail[:, P:SW], ident[:, :]).then_inc(tail_T, 1)
                pe.wait_ge(carry_T, l + 1)
                pe.transpose(t_ps[:, 1, 0:P], carryT[:, 0, :], ident[:, :]).then_inc(carry_back, 1)
                pe.transpose(t_ps[:, 1, P:P + F], carryT[0:F, 1, :], ident[0:F, 0:F]).then_inc(carry_back, 1)

            def sum_tiles(bank, tile, t0, start):
                if known(t0) and t0 == NT - 1:
                    return pe.matmul(h_ps[:, bank, 0:F], ones[0:NL, :], tile[0:NL, NT - 1, :], start=start, stop=True)
                return pe.matmul(h_ps[:, bank, :], ones[:, :], tile[:, bass.ds(t0, 8), :].rearrange("p a b -> p (a b)"), start=start, stop=False)

            def nodes(l):
                def turn(i, s):
                    n = NT * l + s
                    pe.wait_ge(mean_ready, n + 1 + NSLOTS * i)
                    pe.wait_ge(nx_staged, n + 1 + NSLOTS * i)
                    if not is0(i) or l or s >= 2:
                        pe.wait_ge(node_Tc, n - 1 + NSLOTS * i)
                    if is0(i) and s < 2:
                        pe.wait_ge(fix_ready, l + 1)
                    pe.transpose(t_ps[:, s % 2, 0:P], agg[:, s, 0:P], ident[:, :]).then_inc(node_T, 1)
                    pe.transpose(t_ps[:, s % 2, P:2 * P], xp[:, s % XSLOTS, :], ident[:, :]).then_inc(node_T, 1)

                def step(i, s):
                    n = NT * l + s
                    if ahead(i, s, 1, NSLOTS, NT):
                        turn(*ahead(i, s, 1, NSLOTS, NT))
                    pe.wait_ge(node_Tc, n + 1 + NSLOTS * i)
                    if not is0(i) or l or s >= 2:
                        pe.wait_ge(node_done, 2 * n - 2 + 2 * NSLOTS * i)
                    pe.matmul(o_ps[:, s % 2, 0:P], tsb[:, s % 2, 0:P], rw[:, l, 0:2, :].rearrange("p a b -> p (a b)"), start=True, stop=False)
                    pe.matmul(o_ps[:, s % 2, 0:P], tsb[:, s % 2, P:2 * P], rw[:, l, 2:4, :].rearrange("p a b -> p (a b)"), start=False, stop=True).then_inc(node_o, 1)
                    if s == 3 and not is0(i):
                        pe.wait_ge(node_done, 2 * NT * l + 2 * NSLOTS * i)
                        sum_tiles(0, o_all, NSLOTS * (i - 1), known(i) and i == 1)
                turn(0, 0)
                around(pe, NT, NSLOTS, step, head=2)
                pe.wait_ge(node_done, 2 * NT * (l + 1))
                sum_tiles(0, o_all, NT - 1 - 8, False)
                sum_tiles(0, o_all, NT - 1, False).then_inc(mean_ps, 1)

            def squares(l):
                for k, (t0, t1_) in enumerate(norm_chunks):
                    pe.wait_ge(sq_ready, 1 + len(norm_chunks) * l + k + 1)
                    m = sum_tiles(1, x_all, t0, k == 0)
                m.then_inc(var_ps, 1)

            for l in range(LAYERS):
                edges(l)
                if l == 0:
                    log_sum()
                nodes(l)
                squares(l)
                if l + 1 < LAYERS:
                    project(l + 1)


_INS = ["x", "src", "dst", "edge_attr_16", "L0_gnn_We", "L0_gnn_be", "L0_gnn_Wpre", "L0_gnn_bpre", "L0_gnn_Wpost",
        "L0_gnn_bpost", "L0_gnn_Wlin", "L0_gnn_blin", "L0_gnn_gamma", "L0_gnn_beta"]


def kernel(**inputs):
    import numpy as _np
    import concourse.bacc as _bacc
    from concourse import mybir as _mybir
    from concourse.bass_utils import run_bass_kernel_spmd as _run

    nc = _bacc.Bacc("TRN2", target_bir_lowering=False, num_devices=1)
    arrays, args = {}, []
    for name in _INS:
        a = _np.ascontiguousarray(inputs[name])
        arrays[f"in_{name}"] = a
        args.append(nc.dram_tensor(f"in_{name}", a.shape, _mybir.dt.from_np(a.dtype), kind="ExternalInput").ap())
    out = nc.dram_tensor("out_0", (N, F), _mybir.dt.float32, kind="ExternalOutput").ap()
    gnn_program(nc, *args, out)
    r = _run(nc, [arrays], core_ids=[0])
    return r.results[0]["out_0"]
```

```python
import concourse.bass as bass
from concourse import mybir
from contextlib import ExitStack

P = 128
N, F, ED, LAYERS = 6250, 64, 16, 2
E = 206250
GC = 8
COLS = -(-E // P)
NG = -(-COLS // GC)
LASTG = COLS - (NG - 1) * GC
LASTC = E - (P - 1) * COLS
SLOTS = 4
NSLOTS = 8
PSLOTS = 4
XSLOTS = 4
NT = -(-N // P)
NL = N - (NT - 1) * P
CHUNK = 625
NCH = E // CHUNK
ZROW = P * COLS
SW = 3 * F
NEG = GC * ED
CW = NEG + 2 * GC
BIG = 1.0e38
EPS = 1e-5


def gnn_program(nc, x, src, dst, ea, We, be, Wpre, bpre, Wpost, bpost, Wlin, blin, gamma, beta, out):
    f32, i32 = mybir.dt.float32, mybir.dt.int32
    ALU = mybir.AluOpType
    ACT = mybir.ActivationFunctionType
    AX = mybir.AxisListType

    y_dram = nc.dram_tensor("y_rows", (N, F), f32, kind="Internal").ap()
    st_dram = nc.dram_tensor("edge_states", (ZROW + 1, SW), f32, kind="Internal").ap()

    ctx = ExitStack()
    with ctx:
        def sb(name, shape, dt=f32):
            return ctx.enter_context(nc.sbuf_tensor(name, shape, dt))

        def sem(name):
            return ctx.enter_context(nc.semaphore(name))

        comb = sb("comb", [P, NG, NEG + GC])
        src_all = sb("src_all", [P, COLS], i32)
        x_all = sb("x_all", [P, NT, F])
        o_all = sb("o_all", [P, NT, F])
        states = sb("states", [P, SLOTS, GC, SW])
        rows = sb("rows", [P, SLOTS * CHUNK])
        stage = sb("stage", [P, SLOTS, CW])
        idx = sb("idx", [P, SLOTS, GC], i32)
        eaT = sb("eaT", [P, 2, P])
        tsb = sb("tsb", [P, 2, 2 * P])
        xp = sb("xp", [P, XSLOTS, 2 * F])
        ident = sb("ident", [P, P])
        ones = sb("ones", [P, P])
        shiftm = sb("shiftm", [P, P])
        wrapm = sb("wrapm", [P, P])
        bdmask = sb("bdmask", [P, GC])
        bd = sb("bd", [P, LAYERS, GC * F])
        bd1 = sb("bd1", [P, LAYERS, 2 * F])
        rw = sb("rw", [P, LAYERS, 4, F])
        w64 = sb("w64", [F, LAYERS, 2, F])
        we = sb("we", [ED, LAYERS, F])
        bcol = sb("bcol", [F, LAYERS, 2])
        brow = sb("brow", [1, LAYERS, 4, F])
        wide_rows = sb("wide_rows", [P, LAYERS, 5, F])
        nid = sb("nid", [P, NT])
        minus1 = sb("minus1", [P, 1])
        nidh = sb("nidh", [P, NT])
        nidi = sb("nidi", [P, NT], i32)
        le = sb("le", [P, NT])
        chrow = sb("chrow", [P, NT])
        sg = sb("sg", [P, NT])
        ends = sb("ends", [P, NT])
        deg = sb("deg", [P, NT])
        cnt = sb("cnt", [P, NT])
        has = sb("has", [P, NT])
        endf = sb("endf", [P, NT])
        end_i = sb("end_i", [P, NT], i32)
        rcnt = sb("rcnt", [P, NT])
        amp = sb("amp", [P, NT])
        dhi = sb("dhi", [P, 2, NT])
        dint = sb("dint", [P, 3, NT], i32)
        oh = sb("oh", [P, 2, P + NT], mybir.dt.bfloat16)
        small = sb("small", [P, 16])
        fix_i = sb("fix_i", [P, 1], i32)
        pidx_i = sb("pidx_i", [P, 1], i32)
        fixr = sb("fixr", [P, SW])
        links = sb("links", [P, 2, P])
        linkb = sb("linkb", [P, 2, P])
        before = sb("before", [P, 2, P])
        carryT = sb("carryT", [P, 2, P])
        s1 = sb("s1", [P, 4, NT])
        stat = sb("stat", [P, 4, F])
        t1 = sb("t1", [P, 2, F])

        flat = states[:, :, :, :].rearrange("p a b c -> p (a b c)")
        dst_i = flat[:, 0:COLS].bitcast(i32)
        dst_f = flat[:, COLS:2 * COLS]
        same = flat[:, 2 * COLS:3 * COLS]
        fst = flat[0:1, 3 * COLS:3 * COLS + NCH].bitcast(i32)
        fstf = flat[0:1, 3 * COLS + NCH:3 * COLS + 2 * NCH]
        first_b = flat[:, 3 * COLS + 2 * NCH:3 * COLS + 3 * NCH]
        early = stage[:, :, :].rearrange("p a b -> p (a b)")
        wn = early[:, 0:LAYERS * 4 * F].rearrange("p (l a b) -> p l a b", l=LAYERS, a=4)
        iorow = carryT[:, 0, 0:P // 2].bitcast(mybir.dt.bfloat16)
        iorow_i = carryT[:, 1, :].bitcast(i32)
        tsb4 = tsb[:, :, :].rearrange("p a b -> p (a b)").rearrange("p (a b) -> p a b", a=PSLOTS)
        wT = [tsb4[0:F, :, :], xp[0:F, :, :]]
        weT = [linkb[0:F, l, :].rearrange("p (a b) -> p a b", a=GC) for l in range(LAYERS)]
        bcolw = [before[0:F, :, :], links[0:F, :, :]]
        diag2 = tsb[:, 0, :].rearrange("p (a b) -> p a b", a=2)
        zrow = fixr[0:1, :]
        gath = rows[:, 0:SLOTS * GC * F].rearrange("p (s c) -> p s c", s=SLOTS)
        chunks = rows[:, :].bitcast(i32).rearrange("p (s c) -> p s c", s=SLOTS)
        agg = rows[:, 0:NSLOTS * SW].rearrange("p (s c) -> p s c", s=NSLOTS)
        nidx = idx[:, :, :].rearrange("p a b -> p (a b)")

        h_ps = ctx.enter_context(nc.psum_tensor("h_ps", [P, 4, 512], f32))
        t_ps = ctx.enter_context(nc.psum_tensor("t_ps", [P, 2, 512], f32))
        o_ps = ctx.enter_context(nc.psum_tensor("o_ps", [P, 2, 512], f32))

        dst_in, src_in, x_loaded, w_in, fst_in = (sem(n) for n in (
            "dst_in", "src_in", "x_loaded", "w_in", "fst_in"))
        ea_in = [sem(f"ea_in{k}") for k in range(4)]
        zero_in, wpost_in = sem("zero_in"), sem("wpost_in")
        last_log, dve_step, pool_step = sem("last_log"), sem("dve_step"), sem("pool_step")
        first_bc, first_ready = sem("first_bc"), sem("first_ready")
        cidx_ready, chunk_counted, le_done = sem("cidx_ready"), sem("chunk_counted"), sem("le_done")
        chunk_got = [sem(f"chunk_got{s}") for s in range(SLOTS)]
        masks_ready = sem("masks_ready")
        w_t, w_tc, w_p, w_pc = sem("w_t"), sem("w_tc"), sem("w_p"), sem("w_pc")
        ends_ready, starts_ps = sem("ends_ready"), sem("starts_ps")
        onehot_ready, onehot_used = sem("onehot_ready"), sem("onehot_used")
        link_in, link_ps, logs_ready, logsum_ps = sem("link_in"), sem("link_ps"), sem("logs_ready"), sem("logsum_ps")
        x_ready, x_chunk, x_relu, x_scaled, pair_staged, pair_T, pair_Tc, pair_y, pair_yc = (sem(n) for n in (
            "x_ready", "x_chunk", "x_relu", "x_scaled", "pair_staged", "pair_T", "pair_Tc", "pair_y", "pair_yc"))
        y_stored = sem("y_stored")
        idx_staged, const_staged, ea_T, ea_Tc, h_ready, state_done = (sem(n) for n in (
            "idx_staged", "const_staged", "ea_T", "ea_Tc", "h_ready", "state_done"))
        got = [sem(f"got{s}") for s in range(SLOTS)]
        stored = [sem(f"stored{s}") for s in range(SLOTS)]
        tail_T, carry_T, carry_back = sem("tail_T"), sem("carry_T"), sem("carry_back")
        fix_got, fix_ready, fix_stored = sem("fix_got"), sem("fix_ready"), sem("fix_stored")
        nidx_staged, nx_staged, mean_ready, node_T, node_Tc, node_o, node_done = (sem(n) for n in (
            "nidx_staged", "nx_staged", "mean_ready", "node_T", "node_Tc", "node_o", "node_done"))
        agg_got = [sem(f"agg_got{s}") for s in range(NSLOTS)]
        mean_ps, sq_in, sq_ready, var_ps, var_in, std_ready = (sem(n) for n in (
            "mean_ps", "sq_in", "sq_ready", "var_ps", "var_in", "std_ready"))
        turn = sem("turn")
        res_ready, res_stored = sem("res_ready"), sem("res_stored")

        def linker(eng, s):
            n = [0]

            def link(ins):
                n[0] += 1
                ins.then_inc(s, 1)
                eng.wait_ge(s, n[0])
            return link

        def around(eng, total, slots, step, head=1, tail=1, between={}):
            full = total // slots
            for n in range(head * slots):
                step(n // slots, n % slots)
            cuts = [*sorted({head, *between}), full - tail]
            for i0, i1 in zip(cuts, cuts[1:]):
                if i0 in between:
                    between[i0]()
                with eng.Fori(i0, i1) as i:
                    for s in range(slots):
                        step(i, s)
            for n in range((full - tail) * slots, total):
                step(n // slots, n % slots)

        def known(i):
            return isinstance(i, int)

        def is0(i):
            return known(i) and i == 0

        def ahead(i, s, k, slots, total):
            if known(i) and slots * i + s + k >= total:
                return None
            return i + (s + k) // slots, (s + k) % slots

        def uses(layer, s, total, slots=SLOTS):
            return layer * len(range(s, total, slots))

        def ea_loads(piece):
            g0, g1 = ea_pieces[piece]
            return 16 * sum((min(g1, c // GC) > g0) + (min(g1, c // GC) < g1 and c % GC > 0) for c in (COLS, COLS, LASTC))

        def columns(i, s):
            return LASTG if known(i) and SLOTS * i + s == NG - 1 else GC

        def rows_got(l, s, i):
            short = GC - LASTG if s == (NG - 1) % SLOTS else 0
            return 16 * (GC * uses(l, s, NG) - short * l + (columns(i, s) - GC) + GC) + 16 * GC * i

        def states_after(l, i, s):
            return 3 * (COLS * l + GC * s + columns(i, s)) + 3 * GC * SLOTS * i

        PAIRS = NT // 2
        STEPS = PAIRS + 1
        ea_pieces = [(0, 16), (16, 64), (64, 128), (128, NG)]
        norm_chunks = [(t, min(t + 8, NT)) for t in range(0, NT, 8)]
        CH = 4
        w_banks = [(2, 3), (0, 1)]
        y_ps = [o_ps[:, 0, :], o_ps[:, 1, :], t_ps[:, 0, :], t_ps[:, 1, :]]
        assert NT == 2 * PAIRS + 1 and NT % NSLOTS == 1 and NCH * CHUNK == E

        def stage_pairs(eng, copy, l, before_put):
            def put(i, s):
                before_put(i, s)
                if known(i) and PSLOTS * i + s == PAIRS:
                    copy(xp[:, s, 0:F], x_all[:, NT - 1, :]).then_inc(pair_staged, 1)
                else:
                    copy(xp[:, s, :], x_all[:, bass.ds(2 * PSLOTS * i + 2 * s, 2), :].rearrange("p a b -> p (a b)")).then_inc(pair_staged, 1)

            def take(i, s):
                n = STEPS * l + s
                k = F if known(i) and PSLOTS * i + s == PAIRS else P
                eng.wait_ge(pair_T, n + 1 + PSLOTS * i)
                if l > 0 or not is0(i):
                    eng.wait_ge(pair_y, n + 1 - PSLOTS + PSLOTS * i)
                copy(tsb4[0:k, s, :], h_ps[0:k, s, 0:P]).then_inc(pair_Tc, 1)

            def first():
                for s in range(PSLOTS):
                    put(0, s)
                take(0, 0)
                take(0, 1)

            def step(i, s):
                if ahead(i, s, PSLOTS, PSLOTS, STEPS):
                    put(i + 1, s)
                if ahead(i, s, 2, PSLOTS, STEPS):
                    take(*ahead(i, s, 2, PSLOTS, STEPS))
            return first, step

        block = ctx.enter_context(nc.Block())

        @block.sync
        def _(sp):
            sp.dma_start(fst[0:1, :], dst.rearrange("(c k) -> k c", k=CHUNK)[0:1, :], allow_slow_non_contiguous=True).then_inc(fst_in, 16)
            sp.wait_ge(pool_step, 4)
            cut = (P - 1) // 16 * 16

            def load_columns(tile, dram, s):
                v = dram[0:(P - 1) * COLS].rearrange("(p c) -> p c", c=COLS)
                sp.dma_start(tile[0:cut, :], v[0:cut, :]).then_inc(s, 16)
                sp.dma_start(tile[cut:P - 1, :], v[cut:P - 1, :]).then_inc(s, 16)
                sp.dma_start(tile[P - 1:P, 0:LASTC], dram[(P - 1) * COLS:E].rearrange("(p c) -> p c", p=1)).then_inc(s, 16)

            body = ea[0:(P - 1) * COLS, :].rearrange("(p c) k -> p (c k)", c=COLS)
            last = ea[(P - 1) * COLS:E, :].rearrange("(p c) k -> p (c k)", p=1)

            def load_ea(piece):
                g0, g1 = ea_pieces[piece]
                for p0, p1, v, cols in ((0, cut, body, COLS), (cut, P - 1, body, COLS), (P - 1, P, last, LASTC)):
                    q0 = 0 if v is body else P - 1
                    gf = min(g1, cols // GC)
                    if gf > g0:
                        sp.dma_start(comb[p0:p1, g0:gf, 0:NEG],
                                     v[p0 - q0:p1 - q0, g0 * NEG:gf * NEG].rearrange("p (g c) -> p g c", c=NEG)).then_inc(ea_in[piece], 16)
                    if gf < g1 and cols % GC:
                        sp.dma_start(comb[p0:p1, gf, 0:cols % GC * ED],
                                     v[p0 - q0:p1 - q0, gf * NEG:cols * ED]).then_inc(ea_in[piece], 16)

            sp.dma_start(o_all[:, 0:NT - 1, :], x[0:(NT - 1) * P, :].rearrange("(t p) f -> p t f", p=P)).then_inc(x_loaded, 16)
            sp.dma_start(o_all[0:NL, NT - 1, :], x[(NT - 1) * P:N, :]).then_inc(x_loaded, 16)
            for l in range(LAYERS):
                sp.dma_start(w64[:, l, 0, :], Wpre[l, F:2 * F, :]).then_inc(w_in, 16)
                sp.dma_start(w64[:, l, 1, :], Wlin[l, :, :]).then_inc(w_in, 16)
                sp.dma_start(we[:, l, :], We[l, :, :]).then_inc(w_in, 16)
                sp.dma_start(bd1[0:F, l, 0:F], Wpre[l, 0:F, :]).then_inc(w_in, 16)
                sp.dma_start(bd1[F:2 * F, l, F:2 * F], Wpre[l, 0:F, :]).then_inc(w_in, 16)
                sp.dma_start(bcol[:, l, 0:1], be[l, :].rearrange("(f o) -> f o", o=1), allow_slow_non_contiguous=True).then_inc(w_in, 16)
                sp.dma_start(bcol[:, l, 1:2], bpost[l, :].rearrange("(f o) -> f o", o=1), allow_slow_non_contiguous=True).then_inc(w_in, 16)
                for k, b in enumerate((bpre, blin, gamma, beta)):
                    sp.dma_start(brow[0:1, l, k, :], b[l:l + 1, :]).then_inc(w_in, 16)
            sp.wait_ge(dve_step, 1)
            for l in range(LAYERS):
                for half, slot, part in ((0, 0, 3), (1, 0, 2), (0, 1, 6), (1, 1, 5), (0, 2, 1), (1, 2, 0), (0, 3, 4)):
                    sp.dma_start(wn[half * F:(half + 1) * F, l, slot, :],
                                 Wpost[l, part * F:(part + 1) * F, :]).then_inc(wpost_in, 16)
            load_columns(dst_i, dst, dst_in)
            load_columns(src_all, src, src_in)
            sp.dma_start(st_dram[ZROW:ZROW + 1, :], zrow[0:1, :]).then_inc(zero_in, 16)

            st_v = st_dram[0:ZROW, :].rearrange("(p c) w -> p c w", c=COLS)
            for l in range(LAYERS):
                third = (NT - 1) // 3
                for t0 in range(0, NT - 1, third):
                    sp.wait_ge(pair_yc, STEPS * l + (t0 + third) // 2)
                    sp.dma_start(y_dram[t0 * P:(t0 + third) * P, :].rearrange("(t p) f -> p t f", p=P),
                                 o_all[:, t0:t0 + third, :]).then_inc(y_stored, 16)
                sp.wait_ge(pair_yc, STEPS * (l + 1))
                sp.dma_start(y_dram[(NT - 1) * P:N, :], o_all[0:NL, NT - 1, :]).then_inc(y_stored, 16)

                def store(i, s):
                    sp.wait_ge(state_done, states_after(l, i, s))
                    c0, k = GC * SLOTS * i + GC * s, columns(i, s)
                    sp.dma_start(st_v[:, bass.ds(c0, k), :], states[:, s, 0:k, :]).then_inc(stored[s], 16)
                if l == 0:
                    sp.wait_ge(chunk_counted, NT)
                    load_ea(0)
                    sp.wait_ge(pool_step, 18)
                around(sp, NG, SLOTS, store, tail=0,
                       between={} if l else {1: lambda: load_ea(1), 6: lambda: load_ea(2), 14: lambda: load_ea(3)})
            sp.wait_ge(var_ps, LAYERS)
            sp.dma_start(x_all[:, 0:NT - 1, :], x[0:(NT - 1) * P, :].rearrange("(t p) f -> p t f", p=P)).then_inc(x_loaded, 16)
            sp.dma_start(x_all[0:NL, NT - 1, :], x[(NT - 1) * P:N, :]).then_inc(x_loaded, 16)
            for k, (t0, t1_) in enumerate(norm_chunks):
                sp.wait_ge(res_ready, k + 1)
                if t1_ < NT:
                    sp.dma_start(out[t0 * P:t1_ * P, :].rearrange("(t p) f -> p t f", p=P), o_all[:, t0:t1_, :]).then_inc(res_stored, 16)
                else:
                    sp.dma_start(out[t0 * P:N, :], o_all[0:NL, t0, :]).then_inc(res_stored, 16)
            sp.wait_ge(res_stored, 16 * len(norm_chunks))
            sp.wait_ge(zero_in, 16)
            for s in range(SLOTS):
                sp.wait_ge(stored[s], 16 * uses(LAYERS, s, NG))
            sp.wait_ge(fix_stored, 16 * LAYERS)

        @block.gpsimd
        def _(pool):
            lg = LASTC // GC
            link = linker(pool, pool_step)
            link(pool.memset(dst_i[96:P, LASTC:COLS], 8191))
            link(pool.memset(src_all[96:P, LASTC:COLS], 0))
            link(pool.memset(o_all[96:P, NT - 1, :], 0.0))
            link(pool.memset(bd1[:, :, :], 0.0))
            link(pool.iota(nidi[:, :], pattern=[[P, NT]], base=0, channel_multiplier=1))
            link(pool.iota(iorow_i[:, :], pattern=[[1, P]], base=0, channel_multiplier=0))
            link(pool.iota(pidx_i[:, :], pattern=[[0, 1]], base=0, channel_multiplier=1))
            link(pool.memset(ident[:, :], 0.0))
            link(pool.memset(shiftm[:, :], 0.0))
            link(pool.memset(wrapm[:, :], 0.0))
            link(pool.memset(bdmask[:, :], 1.0))
            link(pool.affine_select(out=ident[:, :], in_=ident[:, :], compare_op=ALU.not_equal, fill=1.0,
                               base=0, pattern=[[-1, P]], channel_multiplier=1))
            link(pool.affine_select(out=shiftm[:, :], in_=shiftm[:, :], compare_op=ALU.not_equal, fill=1.0,
                               base=-1, pattern=[[1, P]], channel_multiplier=-1))
            link(pool.affine_select(out=wrapm[:, :], in_=wrapm[:, :], compare_op=ALU.not_equal, fill=1.0,
                               base=1 - P, pattern=[[-1, P]], channel_multiplier=1))
            link(pool.affine_select(out=bdmask[:, :], in_=bdmask[:, :], compare_op=ALU.is_ge, fill=0.0,
                               base=0, pattern=[[-ED, GC]], channel_multiplier=1))
            link(pool.affine_select(out=bdmask[:, :], in_=bdmask[:, :], compare_op=ALU.is_ge, fill=0.0,
                               base=ED - 1, pattern=[[ED, GC]], channel_multiplier=-1))

            link(pool.memset(comb[:, NG - 1, :], 0.0))

            dst_ch = dst.rearrange("(c k) -> c k", k=CHUNK)

            def chunk(i, s):
                pool.wait_ge(cidx_ready, SLOTS * i + s + 1)
                if not is0(i):
                    pool.wait_ge(chunk_counted, SLOTS * (i - 1) + s + 1)
                pool.sem_inc(turn, 1)
                pool.indirect_dma_start(chunks[:, s, :], None, dst_ch,
                                        bass.IndirectOffsetOnAxis(ap=idx[:, s, 0:1], axis=0)).then_inc(chunk_got[s], 16)
            around(pool, NT, SLOTS, chunk, tail=0)
            link(pool.memset(comb[96:P, LASTC // GC:NG - 1, 0:NEG], 0.0))

            for l in range(LAYERS):
                pool.wait_ge(y_stored, 64 * (l + 1))
                if l == 0:
                    pool.wait_ge(chunk_counted, NT)
                else:
                    pool.wait_ge(node_T, 2 * NT * l)
                    pool.wait_ge(mean_ready, NT * l)

                def gather(i, s):
                    pool.wait_ge(idx_staged, NG * l + s + 1 + SLOTS * i)
                    if not is0(i):
                        pool.wait_ge(h_ready, NG * l + s + 1 + SLOTS * (i - 1))
                    pool.sem_inc(turn, 1)
                    for c in range(columns(i, s)):
                        pool.indirect_dma_start(gath[:, s, c * F:(c + 1) * F], None, y_dram,
                                                bass.IndirectOffsetOnAxis(ap=idx[:, s, c:c + 1], axis=0)).then_inc(got[s], 16)
                around(pool, NG, SLOTS, gather, tail=0)

                for s in range(SLOTS):
                    pool.wait_ge(stored[s], 16 * uses(l + 1, s, NG))
                pool.wait_ge(zero_in, 16)
                pool.indirect_dma_start(fixr[:, :], None, st_dram,
                                        bass.IndirectOffsetOnAxis(ap=fix_i[:, 0:1], axis=0)).then_inc(fix_got, 16)
                pool.wait_ge(fix_ready, l + 1)
                pool.indirect_dma_start(st_dram, bass.IndirectOffsetOnAxis(ap=fix_i[:, 0:1], axis=0),
                                        fixr[:, :], None).then_inc(fix_stored, 16)
                pool.wait_ge(fix_stored, 16 * (l + 1))
                pool.wait_ge(h_ready, NG * (l + 1))

                def node_rows(i, s):
                    n = NT * l + s
                    pool.wait_ge(nidx_staged, n + 1 + NSLOTS * i)
                    if not is0(i):
                        pool.wait_ge(node_T, 2 * (n + 1) + 2 * NSLOTS * (i - 1))
                        pool.wait_ge(mean_ready, n + 1 + NSLOTS * (i - 1))
                    pool.sem_inc(turn, 1)
                    pool.indirect_dma_start(agg[:, s, :], None, st_dram,
                                            bass.IndirectOffsetOnAxis(ap=nidx[:, s:s + 1], axis=0)).then_inc(agg_got[s], 16)
                around(pool, NT, NSLOTS, node_rows, tail=0)

        @block.scalar
        def _(act):
            def stage_chunk(i, s):
                act.wait_ge(le_done, SLOTS * i + s + 1)
                act.activation(idx[:, s, 0:1], le[:, bass.ds(SLOTS * i + s, 1)], ACT.Relu, bias=minus1[:, 0:1]).then_inc(cidx_ready, 1)

            def count(i, s):
                act.wait_ge(chunk_got[s], 16 * i + 16)
                t = SLOTS * i + s
                act.activation(chunks[:, s, :].bitcast(f32), chunks[:, s, :], ACT.Sign, bias=nidh[:, bass.ds(t, 1)],
                               scale=-1.0, accum_out=sg[:, bass.ds(t, 1)]).then_inc(chunk_counted, 1)

            def chunk_step(i, s):
                count(i, s)
                if ahead(i, s, SLOTS, SLOTS, NT):
                    stage_chunk(i + 1, s)

            full, half = NT // SLOTS, 5
            for s in range(SLOTS):
                stage_chunk(0, s)
            for s in range(SLOTS):
                chunk_step(0, s)
            with act.Fori(1, half) as i:
                for s in range(SLOTS):
                    chunk_step(i, s)
            act.wait_ge(sq_in, 1)
            act.activation(o_all[:, :, :], x_all[:, :, :], ACT.Square).then_inc(sq_ready, 1)
            for s in range(SLOTS):
                chunk_step(half, s)
            act.wait_ge(var_in, 1)
            act.activation(s1[:, 2, :], s1[:, 1, :], ACT.Sqrt).then_inc(std_ready, 1)
            with act.Fori(half + 1, full - 1) as i:
                for s in range(SLOTS):
                    chunk_step(i, s)
            for n in range((full - 1) * SLOTS, NT):
                chunk_step(n // SLOTS, n % SLOTS)

            def edges(l):
                def stage_idx(i, s):
                    k = columns(i, s)
                    act.copy(idx[:, s, 0:k], src_all[:, bass.ds(GC * SLOTS * i + GC * s, k)]).then_inc(idx_staged, 1)

                def stage_const(i, s):
                    g = bass.ds(SLOTS * i + s, 1)
                    act.copy(stage[:, s, 0:NEG + GC], comb[:, g, :].rearrange("p o c -> p (o c)"))
                    act.activation(stage[:, s, NEG + GC:CW], comb[:, g, NEG:NEG + GC].rearrange("p o c -> p (o c)"),
                                   ACT.Copy, bias=-BIG, scale=BIG).then_inc(const_staged, 1)

                def take(i, s):
                    n = NG * l + s + SLOTS * i
                    act.wait_ge(ea_T, n + 1)
                    if l > 0 or not is0(i) or s >= 2:
                        act.wait_ge(h_ready, n - 1)
                    act.copy(eaT[:, s % 2, :], t_ps[:, s % 2, 0:P]).then_inc(ea_Tc, 1)
                for s in range(SLOTS):
                    stage_idx(0, s)
                if l == 0:
                    act.wait_ge(masks_ready, 1 + (LASTG < GC))
                    act.wait_ge(ea_in[0], ea_loads(0))
                for s in range(SLOTS):
                    stage_const(0, s)
                take(0, 0)

                def step(i, s):
                    if ahead(i, s, 1, SLOTS, NG):
                        take(*ahead(i, s, 1, SLOTS, NG))
                    if ahead(i, s, SLOTS, SLOTS, NG):
                        act.wait_ge(got[s], rows_got(l, s, i))
                        stage_idx(i + 1, s)
                        act.wait_ge(state_done, states_after(l, i, s))
                        stage_const(i + 1, s)
                around(act, NG, SLOTS, step, between={} if l else {
                    g0 // SLOTS - 1: (lambda k: lambda: act.wait_ge(ea_in[k], ea_loads(k)))(k)
                    for k, (g0, _) in enumerate(ea_pieces) if k})

            def nodes(l):
                def stage_idx(i, s):
                    act.copy(nidx[:, s:s + 1], end_i[:, bass.ds(NSLOTS * i + s, 1)]).then_inc(nidx_staged, 1)

                def stage_x(i, s):
                    act.copy(xp[:, s % XSLOTS, F:2 * F], x_all[:, bass.ds(NSLOTS * i + s, 1), :].rearrange("p o c -> p (o c)")).then_inc(nx_staged, 1)

                for s in range(SLOTS):
                    act.wait_ge(got[s], rows_got(l, s, (NG - 1 - s) // SLOTS))
                for s in range(NSLOTS):
                    stage_idx(0, s)
                for s in range(XSLOTS):
                    stage_x(0, s)

                def step(i, s):
                    n = NT * l + s
                    act.wait_ge(node_T, 2 * n + 2 + 2 * NSLOTS * i)
                    if l > 0 or not is0(i) or s >= 2:
                        act.wait_ge(node_o, n - 1 + NSLOTS * i)
                    act.copy(tsb[:, s % 2, :], t_ps[:, s % 2, 0:2 * P]).then_inc(node_Tc, 1)
                    if ahead(i, s, XSLOTS, NSLOTS, NT):
                        stage_x(*ahead(i, s, XSLOTS, NSLOTS, NT))
                    if ahead(i, s, NSLOTS, NSLOTS, NT):
                        stage_idx(i + 1, s)
                around(act, NT, NSLOTS, step)

            def logs():
                act.wait_ge(onehot_used, NT)
                act.activation(small[:, 8:9], o_ps[:, 0, NT - 1:NT], ACT.Ln, bias=1.0).then_inc(last_log, 1)
                act.activation(dhi[:, 0, 0:NT - 1], o_ps[:, 0, 0:NT - 1], ACT.Ln, bias=1.0, accum_out=small[:, 9:10]).then_inc(logs_ready, 1)
                act.activation(amp[:, :], cnt[:, :], ACT.Ln, bias=1.0).then_inc(logs_ready, 1)

            def norm(l):
                for k, (t0, t1_) in enumerate(norm_chunks):
                    act.wait_ge(sq_in, 1 + len(norm_chunks) * l + k + 1)
                    act.activation(x_all[:, t0:t1_, :], o_all[:, t0:t1_, :], ACT.Square).then_inc(sq_ready, 1)
                act.wait_ge(var_in, l + 2)
                act.activation(stat[:, 2, :], stat[:, 1, :], ACT.Sqrt).then_inc(std_ready, 1)

            def project(l):
                def relu(i, s):
                    if s % 2:
                        return
                    c = 2 * i + s // 2
                    act.wait_ge(x_chunk, c + 1)
                    k = 1 if known(c) and CH * c == NT - 1 else CH
                    tiles = bass.ds(2 * PSLOTS * i + 2 * s, k)
                    act.activation(x_all[:, tiles, :], o_all[:, tiles, :], ACT.Relu).then_inc(x_relu, 1)
                    act.wait_ge(x_relu, c + 1)
                    act.sem_inc(turn, 1)
                first, step = stage_pairs(act, act.copy, l, relu)
                first()
                around(act, STEPS, PSLOTS, step)

            act.wait_ge(src_in, 48)
            for l in range(LAYERS):
                edges(l)
                if l == 0:
                    logs()
                nodes(l)
                norm(l)
                if l + 1 < LAYERS:
                    project(l + 1)

        @block.vector
        def _(dve):
            link = linker(dve, dve_step)

            def wide(ap):
                return ap.unsqueeze(2).broadcast_to([P, NT, F])

            dve.memset(ones[:, :], 1.0).then_inc(first_bc, 1)
            dve.memset(minus1[:, :], -1.0)
            dve.memset(zrow[:, :], 0.0)
            link(dve.memset(wn[:, :, 3, :], 0.0))
            dve.wait_ge(fst_in, 16)
            dve.tensor_copy(fstf[0:1, :], fst[0:1, :]).then_inc(first_bc, 1)
            dve.wait_ge(pool_step, 16)
            link(dve.tensor_copy(nid[:, :], nidi[:, :]))
            dve.tensor_scalar(nidh[:, :], nid[:, :], 0.5, None, ALU.add)
            link(dve.tensor_copy(iorow[:, :], iorow_i[:, :]))
            dve.wait_ge(first_ready, 1)
            link(dve.tensor_copy(first_b[:, :], o_ps[:, 0, 0:NCH]))

            def le_step(i, s):
                t = SLOTS * i + s
                if s >= 2 or not is0(i):
                    dve.wait_ge(le_done, t - 1)
                dve.tensor_scalar(o_ps[:, s % 2, 0:NCH], first_b[:, :], nid[:, bass.ds(t, 1)], None,
                                  ALU.is_le, ALU.add, accum_out=le[:, bass.ds(t, 1)]).then_inc(le_done, 1)
            around(dve, NT, SLOTS, le_step, tail=0)
            dve.wait_ge(x_loaded, 32)
            link(dve.tensor_reduce(s1[:, 0, :], o_all[:, :, :], AX.X, ALU.add))
            link(dve.tensor_scalar(s1[:, 0, :], s1[:, 0, :], 1.0 / F, None, ALU.mult))
            dve.tensor_tensor(x_all[:, :, :], o_all[:, :, :], wide(s1[:, 0, :]), ALU.subtract).then_inc(sq_in, 1)
            dve.wait_ge(w_in, 16 * 11 * LAYERS)
            for l in range(LAYERS):
                dve.tensor_copy(bcolw[l], bcol[:, l, :].unsqueeze(2).broadcast_to([F, 2, P]))
                dve.wait_ge(w_t, l + 1)
                dve.tensor_copy(weT[l], t_ps[0:F, l, 0:ED].unsqueeze(1).broadcast_to([F, GC, ED]))
                dve.tensor_copy(wT[l], h_ps[0:F, l, :].rearrange("p (a b) -> p a b", a=4)).then_inc(w_tc, 1)
            dve.wait_ge(sq_ready, 1)
            link(dve.tensor_reduce(s1[:, 1, :], o_all[:, :, :], AX.X, ALU.add))
            dve.tensor_scalar(s1[:, 1, :], s1[:, 1, :], 1.0 / F, EPS, ALU.mult, ALU.add).then_inc(var_in, 1)
            dve.wait_ge(std_ready, 1)
            link(dve.reciprocal(s1[:, 3, :], s1[:, 2, :]))
            link(dve.tensor_tensor(x_all[:, :, :], x_all[:, :, :], wide(s1[:, 3, :]), ALU.mult))
            dve.tensor_scalar(x_all[:, :, :], x_all[:, :, :], 0.0, None, ALU.max).then_inc(x_ready, 1)

            for l in range(LAYERS):
                a, b = w_banks[l]
                dve.wait_ge(w_p, l + 1)
                dve.tensor_tensor(bd[:, l, :].rearrange("p (j f) -> p j f", j=GC),
                                  h_ps[:, a, 0:F].unsqueeze(1).broadcast_to([P, GC, F]),
                                  bdmask[:, :].unsqueeze(2).broadcast_to([P, GC, F]), ALU.mult)
                dve.tensor_copy(rw[:, l, :, :], h_ps[:, b, 0:4 * F].rearrange("p (a b) -> p a b", a=4))
                dve.tensor_copy(wide_rows[:, l, 0:3, :], h_ps[:, a, F:4 * F].rearrange("p (a b) -> p a b", a=3))
                dve.tensor_copy(wide_rows[:, l, 3:5, :], h_ps[:, b, 4 * F:6 * F].rearrange("p (a b) -> p a b", a=2)).then_inc(w_pc, 1)

            def y_out(l, i, s):
                dve.wait_ge(pair_y, STEPS * l + s + 1 + PSLOTS * i)
                k = 1 if known(i) and PSLOTS * i + s == PAIRS else 2
                dve.tensor_tensor(o_all[:, bass.ds(2 * PSLOTS * i + 2 * s, k), :].rearrange("p a b -> p (a b)"), y_ps[s][:, 0:k * F],
                                  wide_rows[:, l, 0:k, :].rearrange("p a b -> p (a b)"), ALU.add).then_inc(pair_yc, 1)

            dve.wait_ge(x_ready, 1)
            dve.wait_ge(w_pc, LAYERS)
            first, pair_step = stage_pairs(dve, dve.tensor_copy, 0, lambda i, s: None)
            first()

            def first_y(i, s):
                pair_step(i, s)
                y_out(0, i, s)
            around(dve, STEPS, PSLOTS, first_y)

            dve.wait_ge(dst_in, 48)
            link(dve.tensor_copy(dst_f[:, :], dst_i[:, :]))
            dve.memset(same[:, 0:1], 0.0)
            link(dve.tensor_tensor(same[:, 1:COLS], dst_f[:, 1:COLS], dst_f[:, 0:COLS - 1], ALU.is_equal))
            gf = COLS // GC
            dve.tensor_copy(comb[:, 0:gf, NEG:NEG + GC], same[:, 0:gf * GC].rearrange("p (g c) -> p g c", c=GC)).then_inc(masks_ready, 1)
            if gf < NG:
                dve.tensor_copy(comb[:, gf, NEG:NEG + LASTG], same[:, gf * GC:COLS]).then_inc(masks_ready, 1)
            dve.tensor_copy(small[:, 0:1], dst_f[:, 0:1])
            link(dve.tensor_copy(small[:, 1:2], dst_f[:, COLS - 1:COLS]))
            link(dve.tensor_scalar(same, dst_f, small[:, 0:1], None, ALU.is_equal, ALU.add, accum_out=small[:, 2:3]))
            link(dve.tensor_copy(small[:, 3:4], pidx_i[:, 0:1]))
            dve.tensor_scalar(small[:, 4:5], small[:, 3:4], float(COLS), -1.0, ALU.mult, ALU.add)
            link(dve.tensor_scalar(small[:, 12:13], small[:, 3:4], 1.0, None, ALU.min))
            link(dve.tensor_tensor(small[:, 5:6], small[:, 4:5], small[:, 2:3], ALU.add))
            link(dve.tensor_copy(fix_i[:, :], small[:, 5:6]))
            dve.memset(states[:, SLOTS - 1, GC - 1, :], 0.0).then_inc(link_in, 1)
            dve.wait_ge(link_ps, 1)
            link(dve.tensor_copy(small[:, 6:8], o_ps[:, 1, 0:2]))
            dve.tensor_tensor(small[:, 10:11], small[:, 7:8], small[:, 0:1], ALU.is_equal)
            link(dve.tensor_tensor(small[:, 11:12], small[:, 7:8], small[:, 6:7], ALU.is_equal))
            link(dve.tensor_tensor(small[:, 10:11], small[:, 10:11], small[:, 12:13], ALU.mult))
            link(dve.tensor_tensor(small[:, 11:12], small[:, 10:11], small[:, 11:12], ALU.mult))
            dve.tensor_scalar(diag2[:, 0, :], ident[:, :], small[:, 10:11], None, ALU.mult)
            dve.tensor_scalar(diag2[:, 1, :], ident[:, :], small[:, 11:12], None, ALU.mult).then_inc(link_in, 1)
            dve.wait_ge(link_ps, 2)
            link(dve.tensor_copy(links[:, :, :], o_ps[:, 1, 0:2 * P].rearrange("p (a b) -> p a b", a=2)))
            dve.tensor_scalar(linkb[0:F, :, :], links[0:F, :, :], -1.0, BIG, ALU.add, ALU.mult)
            dve.tensor_scalar(linkb[F:P, :, :], links[F:P, :, :], -1.0, -BIG, ALU.add, ALU.mult)
            dve.memset(before[0:F, 0, 0:1], -BIG)
            dve.memset(before[F:P, 0, 0:1], BIG)
            link(dve.memset(before[0:F, 1, 0:1], 0.0))

            dve.wait_ge(chunk_counted, NT)
            link(dve.tensor_scalar(ends[:, :], sg[:, :], float(CHUNK), 0.5, ALU.add, ALU.mult))
            link(dve.tensor_scalar(chrow[:, :], le[:, :], -1.0, 0.0, ALU.add, ALU.max))
            link(dve.tensor_scalar(chrow[:, :], chrow[:, :], float(CHUNK), None, ALU.mult))
            dve.tensor_tensor(ends[:, :], ends[:, :], chrow[:, :], ALU.add).then_inc(ends_ready, 1)
            dve.wait_ge(starts_ps, 1)
            link(dve.tensor_tensor(deg[:, :], ends[:, :], o_ps[:, 1, 0:NT], ALU.subtract))
            dve.tensor_scalar(has[:, :], deg[:, :], 1.0, None, ALU.min)
            dve.tensor_scalar(cnt[:, :], deg[:, :], 1.0, None, ALU.max)
            link(dve.tensor_scalar(endf[:, :], ends[:, :], -1.0 - ZROW, None, ALU.add))
            link(dve.reciprocal(rcnt[:, :], cnt[:, :]))
            link(dve.tensor_tensor(endf[:, :], endf[:, :], has[:, :], ALU.mult))
            link(dve.tensor_scalar(endf[:, :], endf[:, :], float(ZROW), None, ALU.add))
            link(dve.tensor_copy(end_i[:, :], endf[:, :]))
            link(dve.tensor_copy(dint[:, 0, :], deg[:, :]))
            dve.tensor_scalar(dint[:, 1, :], dint[:, 0, :], 7, None, ALU.logical_shift_right)
            link(dve.tensor_scalar(dint[:, 2, :], dint[:, 0, :], P - 1, None, ALU.bitwise_and))
            link(dve.tensor_copy(dhi[:, :, :], dint[:, 1:3, :]))

            def one_hot(i, s):
                t = SLOTS * i + s
                if s >= 2 or not is0(i):
                    dve.wait_ge(onehot_used, t - 1)
                dve.tensor_scalar(oh[:, s % 2, 0:P], iorow[:, :], dhi[:, 1, bass.ds(t, 1)], None, ALU.is_equal)
                dve.tensor_scalar(oh[:, s % 2, P:P + NT], iorow[:, 0:NT], dhi[:, 0, bass.ds(t, 1)], None, ALU.is_equal).then_inc(onehot_ready, 1)
            around(dve, NT, SLOTS, one_hot, tail=0)

            def amplify():
                dve.wait_ge(logs_ready, 2)
                dve.wait_ge(logsum_ps, 1)
                link(dve.tensor_reduce(small[:, 13:14], o_ps[:, 1, 0:2], AX.X, ALU.add))
                link(dve.tensor_scalar(small[:, 14:15], small[:, 13:14], 1.0 / N, None, ALU.mult))
                link(dve.reciprocal(small[:, 15:16], small[:, 14:15]))
                link(dve.tensor_scalar(amp[:, :], amp[:, :], small[:, 15:16], None, ALU.mult))

            def edges(l):
                def step(i, s):
                    dve.wait_ge(h_ready, NG * l + s + 1 + SLOTS * i)
                    if l > 0 or not is0(i):
                        dve.wait_ge(stored[s], 16 * uses(l, s, NG) + 16 * i)
                    for c in range(columns(i, s)):
                        n = 3 * (COLS * l + GC * s + c)
                        if l > 0 or not is0(i) or s or c:
                            dve.wait_ge(state_done, n + 3 * GC * SLOTS * i)
                        last = states[:, s, c - 1, :] if c else states[:, (s - 1) % SLOTS, GC - 1, :]
                        h = h_ps[:, s, c * F:(c + 1) * F]
                        one = stage[:, s, NEG + c:NEG + c + 1]
                        neg = stage[:, s, NEG + GC + c:NEG + GC + c + 1]
                        for k, (mask, op0, op1) in enumerate(((neg, ALU.add, ALU.max), (neg, ALU.subtract, ALU.min),
                                                              (one, ALU.mult, ALU.add))):
                            dve.scalar_tensor_tensor(out=states[:, s, c, k * F:(k + 1) * F], in0=last[:, k * F:(k + 1) * F],
                                                     scalar=mask, in1=h, op0=op0, op1=op1).then_inc(state_done, 1)
                around(dve, NG, SLOTS, step, tail=0)

                dve.wait_ge(tail_T, 2 * l + 2)
                dve.tensor_tensor(before[:, 0, 1:P], t_ps[:, 0, 0:P - 1], linkb[:, 0, 1:P], ALU.add)
                link(dve.tensor_tensor(before[0:F, 1, 1:P], t_ps[0:F, 0, P:2 * P - 1], links[0:F, 0, 1:P], ALU.mult))
                dve.tensor_tensor_scan(carryT[0:F, 0, :], linkb[0:F, 1, :], before[0:F, 0, :], -BIG, ALU.add, ALU.max)
                dve.tensor_tensor_scan(carryT[F:P, 0, :], linkb[F:P, 1, :], before[F:P, 0, :], BIG, ALU.add, ALU.min)
                dve.tensor_tensor_scan(carryT[0:F, 1, :], links[0:F, 1, :], before[0:F, 1, :], 0.0, ALU.mult, ALU.add).then_inc(carry_T, 1)
                dve.wait_ge(carry_back, 2 * l + 2)
                dve.wait_ge(fix_got, 16 * (l + 1))
                dve.tensor_tensor(fixr[:, 0:F], fixr[:, 0:F], t_ps[:, 1, 0:F], ALU.max)
                dve.tensor_tensor(fixr[:, F:2 * F], fixr[:, F:2 * F], t_ps[:, 1, F:2 * F], ALU.min)
                dve.tensor_tensor(fixr[:, 2 * F:SW], fixr[:, 2 * F:SW], t_ps[:, 1, 2 * F:SW], ALU.add).then_inc(fix_ready, 1)

            def nodes(l):
                def mean(i, s):
                    n = NT * l + s
                    dve.wait_ge(agg_got[s], 16 * uses(l, s, NT, NSLOTS) + 16 + 16 * i)
                    if l > 0 or not is0(i) or s >= XSLOTS:
                        dve.wait_ge(node_T, 2 * (n + 1 - XSLOTS) + 2 * NSLOTS * i)
                    dve.tensor_scalar(xp[:, s % XSLOTS, 0:F], agg[:, s, 2 * F:SW], rcnt[:, bass.ds(NSLOTS * i + s, 1)], None, ALU.mult).then_inc(mean_ready, 1)

                def output(i, s):
                    n = NT * l + s
                    t = NSLOTS * i + s
                    dve.wait_ge(node_o, n + 1 + NSLOTS * i)
                    dve.scalar_tensor_tensor(out=t1[:, s % 2, :], in0=o_ps[:, s % 2, F:2 * F], scalar=amp[:, bass.ds(t, 1)],
                                             in1=wide_rows[:, l, 2, :], op0=ALU.mult, op1=ALU.add).then_inc(node_done, 1)
                    dve.wait_ge(node_done, 2 * n + 1 + 2 * NSLOTS * i)
                    dve.tensor_tensor(o_all[:, bass.ds(t, 1), :].rearrange("p o c -> p (o c)"), o_ps[:, s % 2, 0:F], t1[:, s % 2, :], ALU.add).then_inc(node_done, 1)

                def step(i, s):
                    if ahead(i, s, 2, NSLOTS, NT):
                        mean(*ahead(i, s, 2, NSLOTS, NT))
                    output(i, s)
                mean(0, 0)
                mean(0, 1)
                around(dve, NT, NSLOTS, step)

            def norm(l, last):
                dve.wait_ge(mean_ps, l + 1)
                link(dve.tensor_reduce(stat[:, 0, :], h_ps[:, 0, :].rearrange("p (a f) -> p f a", f=F), AX.X, ALU.add))
                link(dve.tensor_scalar(stat[:, 0, :], stat[:, 0, :], 1.0 / N, None, ALU.mult))

                def rows_of(ap, k):
                    return ap.unsqueeze(1).broadcast_to([P, k, F])
                for t0, t1_ in norm_chunks:
                    o = o_all[:, t0:t1_, :]
                    dve.tensor_tensor(o, o, rows_of(stat[:, 0, :], t1_ - t0), ALU.subtract).then_inc(sq_in, 1)
                dve.wait_ge(var_ps, l + 1)
                link(dve.tensor_reduce(stat[:, 1, :], h_ps[:, 1, :].rearrange("p (a f) -> p f a", f=F), AX.X, ALU.add))
                dve.tensor_scalar(stat[:, 1, :], stat[:, 1, :], 1.0 / N, EPS, ALU.mult, ALU.add).then_inc(var_in, 1)
                dve.wait_ge(std_ready, l + 2)
                link(dve.reciprocal(stat[:, 3, :], stat[:, 2, :]))
                link(dve.tensor_tensor(stat[:, 3, :], stat[:, 3, :], wide_rows[:, l, 3, :], ALU.mult))
                if last:
                    dve.wait_ge(x_loaded, 64)
                    for t0, t1_ in norm_chunks:
                        o, k = o_all[:, t0:t1_, :], t1_ - t0
                        link(dve.tensor_tensor(o, o, rows_of(stat[:, 3, :], k), ALU.mult))
                        link(dve.tensor_tensor(o, o, rows_of(wide_rows[:, l, 4, :], k), ALU.add))
                        dve.scalar_tensor_tensor(out=o, in0=o, scalar=0.0, in1=x_all[:, t0:t1_, :],
                                                 op0=ALU.max, op1=ALU.add).then_inc(res_ready, 1)
                    return

                def scale(i, s):
                    c = 2 * i + s // 2
                    k = 1 if known(c) and CH * c == NT - 1 else CH
                    o = o_all[:, bass.ds(2 * PSLOTS * i + 2 * s, k), :]
                    dve.tensor_tensor(o, o, rows_of(stat[:, 3, :], k), ALU.mult).then_inc(x_scaled, 1)
                    dve.wait_ge(x_scaled, c + 1)
                    dve.tensor_tensor(o, o, rows_of(wide_rows[:, l, 4, :], k), ALU.add).then_inc(x_chunk, 1)

                def step(i, s):
                    if s % 2 == 0 and ahead(i, s, 6, PSLOTS, STEPS):
                        scale(*ahead(i, s, 6, PSLOTS, STEPS))
                    y_out(l + 1, i, s)
                scale(0, 0)
                scale(0, 2)
                scale(1, 0)
                around(dve, STEPS, PSLOTS, step, tail=2)

            for l in range(LAYERS):
                edges(l)
                if l == 0:
                    amplify()
                nodes(l)
                norm(l, l + 1 == LAYERS)

        @block.tensor
        def _(pe):
            pe.wait_ge(first_bc, 2)
            pe.matmul(o_ps[:, 0, 0:NCH], ones[0:1, :], fstf[0:1, :], start=True, stop=True).then_inc(first_ready, 1)

            pe.wait_ge(pool_step, 16)
            small_loads, row_loads = 11 * LAYERS, 7
            pe.wait_ge(dve_step, 1)
            pe.wait_ge(w_in, 16 * small_loads)
            pe.wait_ge(wpost_in, 16 * row_loads * LAYERS)
            for l in range(LAYERS):
                pe.transpose(t_ps[0:F, l, 0:ED], we[:, l, :], ident[0:ED, 0:ED])
                for k in range(4):
                    t = pe.transpose(h_ps[0:F, l, k * P:(k + 1) * P], wn[:, l, k, :], ident[:, :])
                t.then_inc(w_t, 1)
            pe.wait_ge(w_tc, LAYERS)
            for l in range(LAYERS):
                a, b = w_banks[l]
                pe.matmul(h_ps[:, a, 0:F], weT[l].rearrange("p a b -> p (a b)"), w64[:, l, 0, :], start=True, stop=True)
                for k in range(4):
                    pe.matmul(h_ps[:, b, k * F:(k + 1) * F], wT[l][:, k, :], w64[:, l, 1, :], start=True, stop=True)
                for k, j in enumerate((0, 0, 1)):
                    to = h_ps[:, a, (k + 1) * F:(k + 2) * F]
                    pe.matmul(to, bcolw[l][:, j, :], w64[:, l, j, :], start=True, stop=False)
                    pe.matmul(to, ones[0:1, :], brow[0:1, l, j, :], start=False, stop=True)
                pe.matmul(h_ps[:, b, 4 * F:6 * F], ones[0:1, :], brow[0:1, l, 2:4, :].rearrange("p a b -> p (a b)"), start=True, stop=True).then_inc(w_p, 1)

            def project(l):
                def turn(i, s):
                    n = STEPS * l + s
                    pe.wait_ge(pair_staged, n + 1 + PSLOTS * i)
                    if not is0(i) or l:
                        pe.wait_ge(pair_Tc, n + 1 - PSLOTS + PSLOTS * i)
                    k = F if known(i) and PSLOTS * i + s == PAIRS else P
                    pe.transpose(h_ps[0:k, s, 0:P], xp[:, s, 0:k], ident[:, :]).then_inc(pair_T, 1)

                def step(i, s):
                    n = STEPS * l + s
                    if ahead(i, s, 2, PSLOTS, STEPS):
                        turn(*ahead(i, s, 2, PSLOTS, STEPS))
                    pe.wait_ge(pair_Tc, n + 1 + PSLOTS * i)
                    if not is0(i) or l:
                        pe.wait_ge(pair_yc, n + 1 - PSLOTS + PSLOTS * i)
                    k = F if known(i) and PSLOTS * i + s == PAIRS else P
                    pe.matmul(y_ps[s][:, 0:k], tsb4[0:k, s, :], bd1[0:k, l, 0:k], start=True, stop=True).then_inc(pair_y, 1)
                turn(0, 0)
                turn(0, 1)
                around(pe, STEPS, PSLOTS, step)

            pe.wait_ge(w_pc, LAYERS)
            pe.wait_ge(le_done, NT)
            project(0)

            pe.wait_ge(pair_yc, PAIRS + 1)
            pe.wait_ge(link_in, 1)
            pe.matmul(o_ps[:, 1, 0:2], shiftm[:, :], small[:, 0:2], start=True, stop=True).then_inc(link_ps, 1)
            pe.wait_ge(link_in, 2)
            pe.matmul(o_ps[:, 1, 0:2 * P], ones[:, :], diag2[:, :, :].rearrange("p a b -> p (a b)"), start=True, stop=True).then_inc(link_ps, 1)
            pe.wait_ge(ends_ready, 1)
            pe.matmul(o_ps[:, 1, 0:NT], shiftm[:, :], ends[:, :], start=True, stop=False)
            pe.matmul(o_ps[:, 1, 1:NT], wrapm[:, :], ends[:, 0:NT - 1], start=False, stop=True).then_inc(starts_ps, 1)

            def hist(i, s):
                t = SLOTS * i + s
                pe.wait_ge(onehot_ready, t + 1)
                k = NL if isinstance(i, int) and t == NT - 1 else P
                last = isinstance(i, int) and t == NT - 1
                m = pe.matmul(o_ps[:, 0, 0:NT], oh[0:k, s % 2, 0:P], oh[0:k, s % 2, P:P + NT], start=isinstance(i, int) and t == 0, stop=last)
                m.then_inc(onehot_used, 1)
            around(pe, NT, SLOTS, hist, tail=0)

            def log_sum():
                pe.wait_ge(logs_ready, 2)
                pe.wait_ge(last_log, 1)
                pe.matmul(o_ps[:, 1, 0:1], ones[0:NL, :], small[0:NL, 8:9], start=True, stop=True)
                pe.matmul(o_ps[:, 1, 1:2], ones[:, :], small[:, 9:10], start=True, stop=True).then_inc(logsum_ps, 1)

            def edges(l):
                def turn(i, s):
                    n = NG * l + s + SLOTS * i
                    pe.wait_ge(const_staged, n + 1)
                    if l > 0 or not is0(i) or s >= 2:
                        pe.wait_ge(ea_Tc, n - 1)
                    pe.transpose(t_ps[:, s % 2, 0:P], stage[:, s, 0:NEG], ident[:, :]).then_inc(ea_T, 1)
                pe.wait_ge(pair_yc, STEPS * (l + 1))
                turn(0, 0)

                def step(i, s):
                    if ahead(i, s, 1, SLOTS, NG):
                        turn(*ahead(i, s, 1, SLOTS, NG))
                    pe.wait_ge(ea_Tc, NG * l + s + 1 + SLOTS * i)
                    if not is0(i) or l:
                        if is0(i):
                            pe.wait_ge(state_done, 3 * COLS * l)
                        else:
                            pe.wait_ge(state_done, 3 * (COLS * l + GC * (s + 1)) + 3 * GC * SLOTS * (i - 1))
                    pe.matmul(h_ps[:, s, :], eaT[:, s % 2, :], bd[:, l, :], start=True, stop=False)
                    pe.wait_ge(got[s], rows_got(l, s, i))
                    pe.matmul(h_ps[:, s, :], ident[:, :], gath[:, s, :], start=False, stop=True).then_inc(h_ready, 1)
                around(pe, NG, SLOTS, step)

                tail = states[:, (NG - 1) % SLOTS, LASTG - 1, :]
                pe.wait_ge(state_done, 3 * COLS * (l + 1))
                pe.wait_ge(ea_Tc, NG * (l + 1))
                pe.transpose(t_ps[:, 0, 0:P], tail[:, 0:P], ident[:, :]).then_inc(tail_T, 1)
                pe.transpose(t_ps[0:F, 0, P:2 * P], tail[:, P:SW], ident[:, :]).then_inc(tail_T, 1)
                pe.wait_ge(carry_T, l + 1)
                pe.transpose(t_ps[:, 1, 0:P], carryT[:, 0, :], ident[:, :]).then_inc(carry_back, 1)
                pe.transpose(t_ps[:, 1, P:P + F], carryT[0:F, 1, :], ident[0:F, 0:F]).then_inc(carry_back, 1)

            def sum_tiles(bank, tile, t0, start):
                if known(t0) and t0 == NT - 1:
                    return pe.matmul(h_ps[:, bank, 0:F], ones[0:NL, :], tile[0:NL, NT - 1, :], start=start, stop=True)
                return pe.matmul(h_ps[:, bank, :], ones[:, :], tile[:, bass.ds(t0, 8), :].rearrange("p a b -> p (a b)"), start=start, stop=False)

            def nodes(l):
                def turn(i, s):
                    n = NT * l + s
                    pe.wait_ge(mean_ready, n + 1 + NSLOTS * i)
                    pe.wait_ge(nx_staged, n + 1 + NSLOTS * i)
                    if not is0(i) or l or s >= 2:
                        pe.wait_ge(node_Tc, n - 1 + NSLOTS * i)
                    if is0(i) and s < 2:
                        pe.wait_ge(fix_ready, l + 1)
                    pe.transpose(t_ps[:, s % 2, 0:P], agg[:, s, 0:P], ident[:, :]).then_inc(node_T, 1)
                    pe.transpose(t_ps[:, s % 2, P:2 * P], xp[:, s % XSLOTS, :], ident[:, :]).then_inc(node_T, 1)

                def step(i, s):
                    n = NT * l + s
                    if ahead(i, s, 1, NSLOTS, NT):
                        turn(*ahead(i, s, 1, NSLOTS, NT))
                    pe.wait_ge(node_Tc, n + 1 + NSLOTS * i)
                    if not is0(i) or l or s >= 2:
                        pe.wait_ge(node_done, 2 * n - 2 + 2 * NSLOTS * i)
                    pe.matmul(o_ps[:, s % 2, 0:P], tsb[:, s % 2, 0:P], rw[:, l, 0:2, :].rearrange("p a b -> p (a b)"), start=True, stop=False)
                    pe.matmul(o_ps[:, s % 2, 0:P], tsb[:, s % 2, P:2 * P], rw[:, l, 2:4, :].rearrange("p a b -> p (a b)"), start=False, stop=True).then_inc(node_o, 1)
                    if s == 3 and not is0(i):
                        pe.wait_ge(node_done, 2 * NT * l + 2 * NSLOTS * i)
                        sum_tiles(0, o_all, NSLOTS * (i - 1), known(i) and i == 1)
                turn(0, 0)
                around(pe, NT, NSLOTS, step, head=2)
                pe.wait_ge(node_done, 2 * NT * (l + 1))
                sum_tiles(0, o_all, NT - 1 - 8, False)
                sum_tiles(0, o_all, NT - 1, False).then_inc(mean_ps, 1)

            def squares(l):
                for k, (t0, t1_) in enumerate(norm_chunks):
                    pe.wait_ge(sq_ready, 1 + len(norm_chunks) * l + k + 1)
                    m = sum_tiles(1, x_all, t0, k == 0)
                m.then_inc(var_ps, 1)

            for l in range(LAYERS):
                edges(l)
                if l == 0:
                    log_sum()
                nodes(l)
                squares(l)
                if l + 1 < LAYERS:
                    project(l + 1)


_INS = ["x", "src", "dst", "edge_attr_16", "L0_gnn_We", "L0_gnn_be", "L0_gnn_Wpre", "L0_gnn_bpre", "L0_gnn_Wpost",
        "L0_gnn_bpost", "L0_gnn_Wlin", "L0_gnn_blin", "L0_gnn_gamma", "L0_gnn_beta"]


def kernel(**inputs):
    import numpy as _np
    import concourse.bacc as _bacc
    from concourse import mybir as _mybir
    from concourse.bass_utils import run_bass_kernel_spmd as _run

    nc = _bacc.Bacc("TRN2", target_bir_lowering=False, num_devices=1)
    arrays, args = {}, []
    for name in _INS:
        a = _np.ascontiguousarray(inputs[name])
        arrays[f"in_{name}"] = a
        args.append(nc.dram_tensor(f"in_{name}", a.shape, _mybir.dt.from_np(a.dtype), kind="ExternalInput").ap())
    out = nc.dram_tensor("out_0", (N, F), _mybir.dt.float32, kind="ExternalOutput").ap()
    gnn_program(nc, *args, out)
    r = _run(nc, [arrays], core_ids=[0])
    return r.results[0]["out_0"]
```
